# Optimizing a Trainium2 kernel written in Bass

```python
import numpy as np
import jax
import jax.numpy as jnp

def _softmax(x, axis=-1):
    return jax.nn.softmax(x, axis=axis)

def _gelu(x):
    return jax.nn.gelu(x, approximate=True)

def _silu(x):
    return jax.nn.silu(x)

def _sigmoid(x):
    return jax.nn.sigmoid(x)

def _layernorm(x, axis=-1, eps=1e-05):
    m = jnp.mean(x, axis=axis, keepdims=True)
    v = jnp.var(x, axis=axis, keepdims=True)
    return (x - m) / jnp.sqrt(v + eps)

def _scatter_add(tgt, idx, src, axis=0):
    return tgt.at[idx].add(src)

def _segment_sum(src, seg, n):
    return jax.ops.segment_sum(src, seg, n)
kernel_name = 'mk_vit_tower_d1_tok_img768_r4_2c705b'

def setup_inputs(seed: int=0):
    np.random.seed(seed)
    _w = jnp.asarray

    def _rec_inputs():
        import jax
        import jax.numpy as jnp
        _rk = jax.random.key(seed)
        x = -0.00016672 + 0.999947 * jax.random.normal(jax.random.fold_in(_rk, 1), (32, 3, 96, 96), jnp.float32)
        return x
    x = _rec_inputs()

    def _L0_tok_setup():
        import jax, jax.numpy as jnp
        import numpy as np
        B, C, H, W = (64, 3, 96, 96)
        P = 16
        IN_DIM = C * P * P
        SF_HIDDEN = 768
        EMBED_DIM = 192

        def _patchify(x, p):
            b, c, h, w = x.shape
            nh, nw = (h // p, w // p)
            x = x.reshape(b, c, nh, p, nw, p)
            x = x.transpose(0, 2, 4, 1, 3, 5)
            return x.reshape(b, nh * nw, c * p * p)
        key = jax.random.key(seed)
        k0, k1, k2, k3, k4 = jax.random.split(key, 5)
        scale1 = 1.0 / np.sqrt(IN_DIM)
        scale2 = 1.0 / np.sqrt(SF_HIDDEN)
        return {'x': jax.random.normal(k0, (B, C, H, W), dtype=jnp.float32), 'W1': jax.random.normal(k1, (IN_DIM, SF_HIDDEN), dtype=jnp.float32) * scale1, 'b1': jax.random.normal(k2, (SF_HIDDEN,), dtype=jnp.float32) * scale1, 'W2': jax.random.normal(k3, (SF_HIDDEN, EMBED_DIM), dtype=jnp.float32) * scale2, 'b2': jax.random.normal(k4, (EMBED_DIM,), dtype=jnp.float32) * scale2}
    _L0_tok_all = _L0_tok_setup()
    _L0_tok_in = {k: v for k, v in _L0_tok_all.items() if k in ('W1', 'b1', 'W2', 'b2')}
    del _L0_tok_all

    def _L0_attn_setup():
        import jax, jax.numpy as jnp
        import numpy as np
        HIDDEN = 192
        HEADS = 8
        key = jax.random.key(seed)
        ks = jax.random.split(key, 5)
        b, n = (2, 256)
        x = jax.random.normal(ks[0], (b, n, HIDDEN), dtype=jnp.float32)
        W_qkv = jax.random.normal(ks[1], (HIDDEN, 3 * HIDDEN * HEADS), dtype=jnp.float32) * 0.02
        b_qkv = jnp.zeros((3 * HIDDEN * HEADS,), dtype=jnp.float32)
        W_proj = jax.random.normal(ks[2], (HEADS * HIDDEN, HIDDEN), dtype=jnp.float32) * 0.02
        b_proj = jnp.zeros((HIDDEN,), dtype=jnp.float32)
        return {'x': x, 'W_qkv': W_qkv, 'b_qkv': b_qkv, 'W_proj': W_proj, 'b_proj': b_proj}
    _L0_attn_all = _L0_attn_setup()
    _L0_attn_in = {k: v for k, v in _L0_attn_all.items() if k in ('W_qkv', 'b_qkv', 'W_proj', 'b_proj')}
    del _L0_attn_all

    def _L0_ffn_setup():
        import math
        import jax, jax.numpy as jnp
        import numpy as np
        B, L, D = (8, 1024, 192)
        E = 16
        TOP_K = 2
        F_EXP = 4 * D
        F_SH = F_EXP * 2 // 4
        key = jax.random.key(seed)
        ks = jax.random.split(key, 8)
        s = lambda fan_in: 1.0 / math.sqrt(fan_in)
        return {'hidden_states': jax.random.normal(ks[0], (B, L, D), jnp.float32), 'gate_weight': jax.random.uniform(ks[1], (E, D), jnp.float32, -s(D), s(D)), 'Wg': jax.random.uniform(ks[2], (E, F_EXP, D), jnp.float32, -s(D), s(D)), 'Wu': jax.random.uniform(ks[3], (E, F_EXP, D), jnp.float32, -s(D), s(D)), 'Wd': jax.random.uniform(ks[4], (E, D, F_EXP), jnp.float32, -s(F_EXP), s(F_EXP)), 'Ws_g': jax.random.uniform(ks[5], (F_SH, D), jnp.float32, -s(D), s(D)), 'Ws_u': jax.random.uniform(ks[6], (F_SH, D), jnp.float32, -s(D), s(D)), 'Ws_d': jax.random.uniform(ks[7], (D, F_SH), jnp.float32, -s(F_SH), s(F_SH))}
    _L0_ffn_all = _L0_ffn_setup()
    _L0_ffn_in = {k: v for k, v in _L0_ffn_all.items() if k in ('gate_weight', 'Wg', 'Wu', 'Wd', 'Ws_g', 'Ws_u', 'Ws_d')}
    del _L0_ffn_all
    return {'x': x, 'L0_tok_W1': _L0_tok_in['W1'], 'L0_tok_b1': _L0_tok_in['b1'], 'L0_tok_W2': _L0_tok_in['W2'], 'L0_tok_b2': _L0_tok_in['b2'], 'L0_attn_W_qkv': _L0_attn_in['W_qkv'], 'L0_attn_b_qkv': _L0_attn_in['b_qkv'], 'L0_attn_W_proj': _L0_attn_in['W_proj'], 'L0_attn_b_proj': _L0_attn_in['b_proj'], 'L0_ffn_gate_weight': _L0_ffn_in['gate_weight'], 'L0_ffn_Wg': _L0_ffn_in['Wg'], 'L0_ffn_Wu': _L0_ffn_in['Wu'], 'L0_ffn_Wd': _L0_ffn_in['Wd'], 'L0_ffn_Ws_g': _L0_ffn_in['Ws_g'], 'L0_ffn_Ws_u': _L0_ffn_in['Ws_u'], 'L0_ffn_Ws_d': _L0_ffn_in['Ws_d']}

def reference(x, L0_tok_W1, L0_tok_b1, L0_tok_W2, L0_tok_b2, L0_attn_W_qkv, L0_attn_b_qkv, L0_attn_W_proj, L0_attn_b_proj, L0_ffn_gate_weight, L0_ffn_Wg, L0_ffn_Wu, L0_ffn_Wd, L0_ffn_Ws_g, L0_ffn_Ws_u, L0_ffn_Ws_d):
    import jax
    import jax.numpy as jnp

    def _L0_tok_ref(x, W1, b1, W2, b2):
        import jax, jax.numpy as jnp
        import numpy as np
        B, C, H, W = (64, 3, 96, 96)
        P = 16
        IN_DIM = C * P * P
        SF_HIDDEN = 768
        EMBED_DIM = 192

        def _patchify(x, p):
            b, c, h, w = x.shape
            nh, nw = (h // p, w // p)
            x = x.reshape(b, c, nh, p, nw, p)
            x = x.transpose(0, 2, 4, 1, 3, 5)
            return x.reshape(b, nh * nw, c * p * p)
        tokens = _patchify(x, P)
        h = jax.nn.relu(jnp.einsum('bnd,dh->bnh', tokens, W1) + b1)
        out = jax.nn.relu(jnp.einsum('bnh,he->bne', h, W2) + b2)
        return out

    def _L0_attn_ref(x, W_qkv, b_qkv, W_proj, b_proj):
        import jax, jax.numpy as jnp
        import numpy as np
        HIDDEN = 192
        HEADS = 8
        b, n, c = x.shape
        qkv = x @ W_qkv + b_qkv
        q, k, v = jnp.split(qkv, 3, axis=-1)
        q = q.reshape(b, HEADS, n, HIDDEN)
        k = k.reshape(b, HEADS, n, HIDDEN)
        v = v.reshape(b, HEADS, n, HIDDEN)
        energy = jnp.einsum('bhqd,bhkd->bhqk', q, k)
        scaling = jnp.float32(HIDDEN ** 0.5)
        attn = jax.nn.softmax(energy, axis=-1) / scaling
        out = jnp.einsum('bhal,bhlv->bhav', attn, v)
        out = out.reshape(b, n, HEADS * HIDDEN)
        return out @ W_proj + b_proj

    def _L0_ffn_ref(hidden_states, gate_weight, Wg, Wu, Wd, Ws_g, Ws_u, Ws_d):
        import math
        import jax, jax.numpy as jnp
        import numpy as np
        B, L, D = (8, 1024, 192)
        E = 16
        TOP_K = 2
        F_EXP = 4 * D
        F_SH = F_EXP * 2 // 4
        b, l, d = hidden_states.shape
        n = b * l
        x = hidden_states.reshape(n, d)
        scores = jax.nn.sigmoid(x @ gate_weight.T)
        capacity = math.ceil(n / E * TOP_K)
        topk_score, topk_ids = jax.lax.top_k(scores.T, capacity)
        xg = x[topk_ids]
        gate = jax.nn.silu(jnp.einsum('ecd,efd->ecf', xg, Wg))
        up = jnp.einsum('ecd,efd->ecf', xg, Wu)
        out = jnp.einsum('ecf,edf->ecd', gate * up, Wd)
        out = out * topk_score[..., None]
        y = jnp.zeros((n, d), x.dtype).at[topk_ids.reshape(-1)].add(out.reshape(-1, d))
        y = y.reshape(b, l, d)
        shared = jax.nn.silu(hidden_states @ Ws_g.T) * (hidden_states @ Ws_u.T) @ Ws_d.T
        return y + shared
    h = _L0_tok_ref(x, L0_tok_W1, L0_tok_b1, L0_tok_W2, L0_tok_b2)
    h = h + _L0_attn_ref(_layernorm(h, axis=-1), L0_attn_W_qkv, L0_attn_b_qkv, L0_attn_W_proj, L0_attn_b_proj)
    h = h + _L0_ffn_ref(_layernorm(h, axis=-1), L0_ffn_gate_weight, L0_ffn_Wg, L0_ffn_Wu, L0_ffn_Wd, L0_ffn_Ws_g, L0_ffn_Ws_u, L0_ffn_Ws_d)
    return h

_drawn_inputs = setup_inputs


def setup_inputs(seed=0):
    import zlib

    import numpy as np

    out = dict(_drawn_inputs(seed))
    spreads = {'L0_attn_b_qkv': (0.0, 0.364), 'L0_attn_b_proj': (0.0, 0.1)}
    factors = {}
    for name, (base, spread) in spreads.items():
        noise = np.random.default_rng([zlib.crc32(name.encode()), seed]).standard_normal(out[name].shape)
        drawn = base * np.exp(spread * noise) if base else spread * noise
        out[name] = jnp.asarray(drawn.astype(out[name].dtype))
    for name, factor in factors.items():
        out[name] = (out[name] * factor).astype(out[name].dtype)
    return out
```

```python
from contextlib import ExitStack

import concourse.bass as bass
import concourse.mybir as mybir

F32 = mybir.dt.float32
BF16 = mybir.dt.bfloat16
U32 = mybir.dt.uint32
ACT = mybir.ActivationFunctionType
ALU = mybir.AluOpType
AX = mybir.AxisListType

IMAGES, SEQ, D = 32, 36, 192
N = IMAGES * SEQ
PATCH = 16
IN_DIM = 3 * PATCH * PATCH
HID = 768
HEADS = 8
QKV = HEADS * D
E, F_EXP, TOP_K, F_SH = 16, 768, 2, 384
CAP = N * TOP_K // E
EPS = 1e-5

G = 288
NG = N // G
T = 96
NT = G // T
KI = IN_DIM // 128
KH = HID // 128
DM, DR = 128, D - 128
PAIR = 72
BP = 4
NB = G // 9 // BP
BW = BP * PAIR
NQK = 24
HC = CAP // 2
KF = F_EXP // 128
KS = F_SH // 128
ROUNDS = CAP // 8
LN_LINKS = 13
ds = bass.ds


def wait(eng, sem, value):
    if not isinstance(value, int) or value > 0:
        eng.wait_ge(sem, value)


class Chain:

    def __init__(self, eng, sem, start=0):
        self.eng, self.sem, self.n, self.off = eng, sem, start, 0

    def __call__(self, ins):
        self.n += 1
        ins.then_inc(self.sem, 1)
        self.eng.wait_ge(self.sem, self.off + self.n)

    def loop(self, turn, per):
        self.n, self.per, self.off = 0, per, turn * per

    def end(self):
        assert self.n == self.per, (self.n, self.per)


def layer_norm(dve, link, src, ln, turn, s_var, s_std, xtok_free, s_xtok, spare):
    dve.memset(spare, 0.0)
    for t in range(NT):
        dve.bn_stats(ln["stats"][:, t, :], src(t)).then_inc(ln["s_stat"], 1)
    dve.wait_ge(ln["s_stat"], turn * NT + NT)
    dve.memset(spare, 0.0)
    for t in range(NT - 1):
        dve.bn_aggr(ln["mv"][:, t, :], ln["stats"][:, t, :])
    link(dve.bn_aggr(ln["mv"][:, NT - 1, :], ln["stats"][:, NT - 1, :]))
    ve, std, rs, rt = ln["ve"], ln["std"], ln["rs"], ln["rt"]
    dve.tensor_scalar(ve[:, :], ln["mv"][:, :, 1], EPS, None, ALU.add).then_inc(s_var, 1)
    dve.wait_ge(s_std, turn + 1)
    link(dve.reciprocal(rs[:, :], std[:, :]))
    link(dve.tensor_tensor(rt[:, :], rs[:, :], rs[:, :], ALU.mult))
    link(dve.tensor_tensor(rt[:, :], rt[:, :], ve[:, :], ALU.mult))
    link(dve.tensor_scalar(rt[:, :], rt[:, :], -0.5, 1.5, ALU.mult, ALU.add))
    link(dve.tensor_tensor(rs[:, :], rs[:, :], rt[:, :], ALU.mult))
    xtok_free()
    for t in range(NT):
        ins = dve.tensor_scalar(ln["xtok"][:, t, :], src(t), ln["mv"][:, t, 0:1], rs[:, t:t + 1],
                                ALU.subtract, ALU.mult)
        ins.then_inc(s_xtok, 1)


LN_LINKS = 6


def vit_moe_kernel(nc, xT, W1, b1, W2, b2, Wqk, bqk, Wv, bv, Wp, bp, blocks, gateT, Wgu, Wd, Wsgu, Wsd, out):
    with ExitStack() as ctx:
        def sb(name, shape, dt=F32):
            return ctx.enter_context(nc.sbuf_tensor(name, shape, dt))

        def sem(name):
            return ctx.enter_context(nc.semaphore(name))

        out_rows = out.rearrange("a b c -> (a b) c")
        v_dram = nc.dram_tensor("v_scratch", [N, QKV], F32, kind="Internal").ap()
        x3_dram = nc.dram_tensor("x3_scratch", [N, D], F32, kind="Internal").ap()

        ident = sb("ident", [128, 128])
        h_all = sb("h_all", [T, NG * NT, D])
        x2Tm = sb("x2Tm", [DM, N])
        x2Tr = sb("x2Tr", [DR, N])
        x3Tm = sb("x3Tm", [DM, N])
        x3Tr = sb("x3Tr", [DR, N])
        hsum = sb("hsum", [T, NT, D])
        spare = sb("spare", [1, 1])[:, :]
        pspare = sb("pspare", [1, 2])
        ln = {"stats": sb("stats", [T, NT, 6]), "mv": sb("mv", [T, NT, 2]), "ve": sb("ve", [T, NT]),
              "std": sb("std", [T, NT]), "rs": sb("rs", [T, NT]), "rt": sb("rt", [T, NT]),
              "xtok": sb("xtok", [T, NT, D])}
        xtok, ve, std = ln["xtok"], ln["ve"], ln["std"]

        wqkm = sb("wqkm", [DM, NQK, 128])
        wqkr = sb("wqkr", [DR, NQK, 128])
        bqks = sb("bqks", [128, NQK])
        wpm = sb("wpm", [DM, HEADS, D])
        wpr = sb("wpr", [DR, HEADS, D])
        bps = sb("bps", [T, D])
        blk = sb("blk", [2, 2 * PAIR])

        B = [ctx.enter_context(nc.psum_tensor(f"bank{i}", [128, 512], F32)) for i in range(6)]
        ps67 = ctx.enter_context(nc.psum_tensor("bank67", [128, 1024], F32))
        B += [ps67[:, 0:512], ps67[:, 512:1024]]
        tok_ps = ps67[0:T, 0:NT * 256].rearrange("p (t c) -> p t c", t=NT)[:, :, 0:D]

        s_watt = sem("s_watt")

        with ExitStack() as st:
            def sb(name, shape, dt=F32):
                return st.enter_context(nc.sbuf_tensor(name, shape, dt))

            def sem(name):
                return st.enter_context(nc.semaphore(name))

            xs = sb("xs", [128, NG, KI, G])
            w1 = sb("w1", [128, KH, KI, 128])
            w2 = sb("w2", [128, KH, D])
            b1s = sb("b1s", [128, KH])
            b2s = sb("b2s", [T, D])
            wvm = sb("wvm", [DM, QKV])
            wvr = sb("wvr", [DR, QKV])
            bvs = sb("bvs", [T, QKV])
            hT = sb("hT", [128, KH, G])
            x2gm = sb("x2gm", [DM, G])
            x2gr = sb("x2gr", [DR, G])
            vtok = sb("vtok", [T, NT, QKV])

            s_id = sem("s_id")
            s_x = [sem(f"s_x{g}") for g in range(NG)]
            s_w1 = [sem(f"s_w1_{m}") for m in range(KH)]
            s_small = sem("s_small")
            s_w2v = sem("s_w2v")
            s_tok1 = sem("s_tok1")
            s_hT = sem("s_hT")
            s_tok2 = sem("s_tok2")
            s_hsum = sem("s_hsum")
            s_var = sem("s_var")
            s_std = sem("s_std")
            s_xtok = sem("s_xtok")
            s_x2ps = sem("s_x2ps")
            s_x2a = sem("s_x2a")
            s_x2d = sem("s_x2d")
            s_v = sem("s_v")
            s_vsb = sem("s_vsb")
            s_vout = [sem(f"s_vout{t}") for t in range(NT)]
            s_dve = sem("s_dve")
            ln["s_stat"] = sem("s_stat")
            block = st.enter_context(nc.Block())

            @block.sync
            def _(sp):
                for g in range(NG):
                    sp.dma_start(xs[:, g, :, :], xT[g]).then_inc(s_x[g], 16)
                    if g == 0:
                        for m in range(KH):
                            sp.dma_start(w1[:, m, :, :], W1[m]).then_inc(s_w1[m], 16)
                        sp.dma_start(b1s[:, :], b1).then_inc(s_small, 16)
                        sp.dma_start(b2s[:, :], b2.partition_broadcast(T)).then_inc(s_small, 16)
                        sp.dma_start(bvs[:, :], bv.partition_broadcast(T)).then_inc(s_small, 16)
                        sp.dma_start(w2[:, :, :], W2).then_inc(s_w2v, 16)
                        sp.dma_start(wvm[:, :], Wv[0:DM, :]).then_inc(s_w2v, 16)
                        sp.dma_start(wvr[:, :], Wv[DM:D, :]).then_inc(s_w2v, 16)
                sp.dma_start(wqkm[:, :, :], Wqk[0:DM]).then_inc(s_watt, 16)
                sp.dma_start(wqkr[:, :, :], Wqk[DM:D]).then_inc(s_watt, 16)
                sp.dma_start(bqks[:, :], bqk).then_inc(s_watt, 16)
                sp.dma_start(wpm[:, :, :], Wp[0:DM]).then_inc(s_watt, 16)
                sp.dma_start(wpr[:, :, :], Wp[DM:D]).then_inc(s_watt, 16)
                sp.dma_start(bps[:, :], bp.partition_broadcast(T)).then_inc(s_watt, 16)
                sp.dma_start(blk[:, :], blocks).then_inc(s_watt, 16)
                with sp.Fori(0, NG) as g:
                    for t in range(NT):
                        sp.wait_ge(s_vsb, g * 9 + 3 * t + 3)
                        sp.dma_start(v_dram[ds(g * G + t * T, T), :], vtok[:, t, :]).then_inc(s_vout[t], 16)
                for t in range(NT):
                    sp.wait_ge(s_vout[t], 16 * NG)
                sp.wait_ge(s_watt, 7 * 16)

            @block.gpsimd
            def _(pool):
                pool.memset(pspare[:, :], 0.0)
                pool.memset(ident[:, :], 0.0).then_inc(s_id, 1)
                pool.wait_ge(s_id, 1)
                pool.affine_select(out=ident[:, :], in_=ident[:, :], compare_op=ALU.not_equal, fill=1.0, base=0,
                                   pattern=[[-1, 128]], channel_multiplier=1).then_inc(s_id, 1)

            @block.tensor
            def _(pe):
                def tok1(g):
                    for m in range(KH):
                        if isinstance(g, int) and g == 0:
                            pe.wait_ge(s_w1[m], 16)
                        wait(pe, s_hT, g * KH + m - 1)
                        for k in range(KI):
                            x = xs[:, ds(g, 1), k, :].rearrange("p a b -> p (a b)")
                            ins = pe.matmul(B[m % 2][:, 0:G], w1[:, m, k, :], x, start=(k == 0), stop=(k == KI - 1))
                        ins.then_inc(s_tok1, 1)

                def tok2(g):
                    pe.wait_ge(s_hT, g * KH + KH)
                    wait(pe, s_hsum, g)
                    for t in range(NT):
                        for k in range(KH):
                            ins = pe.matmul(tok_ps[:, t, :], hT[:, k, t * T:(t + 1) * T], w2[:, k, :],
                                            start=(k == 0), stop=(k == KH - 1))
                    ins.then_inc(s_tok2, 1)

                def turn_and_v(g):
                    pe.wait_ge(s_xtok, g * NT + NT)
                    wait(pe, s_x2a, g * 2)
                    wait(pe, s_x2d, g * 2)
                    for t in range(NT):
                        pe.transpose(B[2][:, t * T:(t + 1) * T], xtok[:, t, 0:DM], ident[0:T, 0:T])
                    for t in range(NT):
                        ins = pe.transpose(B[3][0:DR, t * T:(t + 1) * T], xtok[:, t, DM:D], ident[0:T, 0:T])
                    ins.then_inc(s_x2ps, 1)
                    pe.wait_ge(s_x2a, g * 2 + 1)
                    pe.wait_ge(s_x2d, g * 2 + 1)
                    for t in range(NT):
                        for c in range(3):
                            i = 3 * t + c
                            wait(pe, s_vsb, g * 9 + (i - 1 if i else 0))
                            o = B[4 + i % 2][0:T, :]
                            cs = slice(c * 512, (c + 1) * 512)
                            pe.matmul(o, x2gm[:, t * T:(t + 1) * T], wvm[:, cs], start=True, stop=False)
                            pe.matmul(o, x2gr[:, t * T:(t + 1) * T], wvr[:, cs],
                                      start=False, stop=True).then_inc(s_v, 1)

                pe.wait_ge(s_x[0], 16)
                tok1(0)
                pe.wait_ge(s_w2v, 48)
                pe.wait_ge(s_id, 2)
                for g in range(1, NG):
                    pe.wait_ge(s_x[g], 16)
                tok2(0)
                tok1(1)
                turn_and_v(0)
                with pe.Fori(1, NG - 1) as g:
                    tok2(g)
                    tok1(g + 1)
                    turn_and_v(g)
                tok2(NG - 1)
                turn_and_v(NG - 1)

            @block.scalar
            def _(act):
                def hidden(g, m):
                    act.wait_ge(s_tok1, g * KH + m + 1)
                    act.activation(hT[:, m, :], B[m % 2][:, 0:G], ACT.Relu, bias=b1s[:, m:m + 1]).then_inc(s_hT, 1)

                def root(g):
                    act.wait_ge(s_var, g + 1)
                    act.activation(std[:, :], ve[:, :], ACT.Sqrt).then_inc(s_std, 1)

                def turned(g):
                    act.wait_ge(s_x2ps, g + 1)
                    act.activation(x2gm[:, :], B[2][:, 0:G], ACT.Copy).then_inc(s_x2a, 1)
                    act.activation(x2Tm[:, ds(g * G, G)], B[2][:, 0:G], ACT.Copy).then_inc(s_x2a, 1)

                act.wait_ge(s_small, 48)
                for m in range(KH):
                    hidden(0, m)
                with act.Fori(0, NG - 1) as g:
                    hidden(g + 1, 0)
                    root(g)
                    for m in range(1, KH):
                        hidden(g + 1, m)
                    turned(g)
                root(NG - 1)
                turned(NG - 1)

            @block.vector
            def _(dve):
                link = Chain(dve, s_dve)
                dve.wait_ge(s_small, 48)

                def group(g):
                    link.loop(g, LN_LINKS + 1)
                    dve.wait_ge(s_tok2, g + 1)
                    dve.tensor_tensor(hsum[:, :, :], tok_ps, b2s[:, None, :].broadcast_to([T, NT, D]),
                                      ALU.add).then_inc(s_hsum, 1)
                    dve.wait_ge(s_hsum, g + 1)
                    link(dve.tensor_scalar(h_all[:, ds(g * NT, NT), :], hsum[:, :, :], 0.0, None, ALU.max))

                    def xtok_free():
                        wait(dve, s_x2ps, g)

                    layer_norm(dve, link, lambda t: h_all[:, ds(g * NT + t, 1), :].rearrange("p a d -> p (a d)"),
                               ln, g, s_var, s_std, xtok_free, s_xtok, spare)
                    dve.wait_ge(s_x2ps, g + 1)
                    dve.tensor_copy(x2gr[:, :], B[3][0:DR, 0:G]).then_inc(s_x2d, 1)
                    dve.tensor_copy(x2Tr[:, ds(g * G, G)], B[3][0:DR, 0:G]).then_inc(s_x2d, 1)
                    for t in range(NT):
                        wait(dve, s_vout[t], g * 16)
                        for c in range(3):
                            i = 3 * t + c
                            cs = slice(c * 512, (c + 1) * 512)
                            dve.wait_ge(s_v, g * 9 + i + 1)
                            dve.tensor_tensor(vtok[:, t, cs], B[4 + i % 2][0:T, :], bvs[:, cs],
                                              ALU.add).then_inc(s_vsb, 1)
                    link.end()

                group(0)
                with dve.Fori(1, NG) as g:
                    group(g)

        with ExitStack() as st:
            def sb(name, shape, dt=F32):
                return st.enter_context(nc.sbuf_tensor(name, shape, dt))

            def sem(name):
                return st.enter_context(nc.semaphore(name))

            qm = sb("qm", [DM, G, HEADS])
            qr = sb("qr", [DR, G, HEADS])
            km = sb("km", [DM, G, HEADS])
            kr = sb("kr", [DR, G, HEADS])
            vp = sb("vp", [PAIR, NB * BP, D])
            om = sb("om", [DM, G, HEADS])
            orr = sb("orr", [DR, G, HEADS])
            pr = sb("pr", [PAIR, 2, BP, PAIR])
            pt = sb("pt", [PAIR, 2, BW])
            mx = sb("mx", [PAIR, 2, BP])
            sm = sb("sm", [PAIR, 2, BP])
            ri = sb("ri", [PAIR, 2, BP])
            blkb = sb("blkb", [2, 2 * PAIR], BF16)

            s_blk = sem("s_blk")
            s_qk = sem("s_qk")
            s_qka = sem("s_qka")
            s_qkd = sem("s_qkd")
            s_vin = sem("s_vin")
            s_e = sem("s_e")
            s_max = sem("s_max")
            s_sub = sem("s_sub")
            s_exp = sem("s_exp")
            s_sum = sem("s_sum")
            s_rec = sem("s_rec")
            s_prob = sem("s_prob")
            s_at = sem("s_at")
            s_atsb = sem("s_atsb")
            s_o = sem("s_o")
            s_oa = sem("s_oa")
            s_od = sem("s_od")
            s_proj = sem("s_proj")
            s_hsum = sem("s_hsum2")
            s_var = sem("s_var2")
            s_std = sem("s_std2")
            s_xtok = sem("s_xtok2")
            s_x3out = sem("s_x3out")
            s_dve = sem("s_dve2")
            ln["s_stat"] = sem("s_stat2")
            block = st.enter_context(nc.Block())

            RING = NQK + 2
            HALF = RING // 2

            def items(g):
                return g * RING - 2 if not isinstance(g, int) or g > 0 else 0

            def halves(g):
                return g * HALF - 1 if not isinstance(g, int) or g > 0 else 0

            @block.sync
            def _(sp):

                def group(g):
                    wait(sp, s_o, g * NB)
                    sp.dma_start(vp[:, :, :], v_dram[ds(g * G, G), :].rearrange(
                        "(n t) (j d) -> (t j) n d", t=9, j=HEADS)).then_inc(s_vin, 16)
                    sp.wait_ge(s_xtok, g * NT + NT)
                    for t in range(NT):
                        sp.dma_start(x3_dram[ds(g * G + t * T, T), :], xtok[:, t, :]).then_inc(s_x3out, 16)

                group(0)
                with sp.Fori(1, NG) as g:
                    group(g)
                sp.wait_ge(s_x3out, 16 * NT * NG)

            @block.tensor
            def _(pe):
                def ring_free(g, i):
                    done = i // 2
                    if isinstance(g, int) and halves(g) + done == 0:
                        return
                    pe.wait_ge(s_qka if i % 2 == 0 else s_qkd, halves(g) + done)

                def x3_turn(g, at):
                    pe.wait_ge(s_xtok, g * NT + NT)
                    ring_free(g + 1, at)
                    ring_free(g + 1, at + 1)
                    for t in range(NT):
                        ins = pe.transpose(B[0][:, t * T:(t + 1) * T], xtok[:, t, 0:DM], ident[0:T, 0:T])
                    ins.then_inc(s_qk, 1)
                    for t in range(NT):
                        ins = pe.transpose(B[1][0:DR, t * T:(t + 1) * T], xtok[:, t, DM:D], ident[0:T, 0:T])
                    ins.then_inc(s_qk, 1)

                def scores(g, b):
                    if not isinstance(g, int) or g or b >= 2:
                        pe.wait_ge(s_sub, g * NB + b - 1)
                    for p in range(BP):
                        o = B[2 + b % 2][0:PAIR, p * PAIR:(p + 1) * PAIR]
                        ts = slice((b * BP + p) * 9, (b * BP + p + 1) * 9)
                        pe.matmul(o, blkb[:, 0:PAIR], blkb[:, PAIR:2 * PAIR], start=True, stop=False)
                        pe.matmul(o, qm[:, ts, :].rearrange("p t j -> p (t j)"),
                                  km[:, ts, :].rearrange("p t j -> p (t j)"), start=False, stop=False)
                        ins = pe.matmul(o, qr[:, ts, :].rearrange("p t j -> p (t j)"),
                                        kr[:, ts, :].rearrange("p t j -> p (t j)"), start=False, stop=True)
                    ins.then_inc(s_e, 1)

                def turn_probs(g, b):
                    pe.wait_ge(s_prob, g * NB + b + 1)
                    if not isinstance(g, int) or g or b >= 2:
                        pe.wait_ge(s_atsb, g * NB + b - 1)
                    for p in range(BP):
                        ins = pe.transpose(B[4 + b % 2][0:PAIR, p * PAIR:(p + 1) * PAIR], pr[:, b % 2, p, :],
                                           ident[0:PAIR, 0:PAIR])
                    ins.then_inc(s_at, 1)

                def weigh(g, b):
                    pe.wait_ge(s_atsb, g * NB + b + 1)
                    if not isinstance(g, int) or g or b:
                        pe.wait_ge(s_oa, g * NB + b)
                        pe.wait_ge(s_od, g * NB + b)
                    for p in range(BP):
                        cs = slice(p * PAIR, (p + 1) * PAIR)
                        pe.matmul(B[6][:, cs], vp[:, b * BP + p, 0:DM], pt[:, b % 2, cs], start=True, stop=True)
                        ins = pe.matmul(B[7][0:DR, cs], vp[:, b * BP + p, DM:D], pt[:, b % 2, cs],
                                        start=True, stop=True)
                    ins.then_inc(s_o, 1)

                def group(g):
                    first = isinstance(g, int)
                    for i in range(NQK):
                        ring_free(g, i)
                        pe.matmul(B[i % 2][:, 0:G], wqkm[:, i, :], x2Tm[:, ds(g * G, G)], start=True, stop=False)
                        pe.matmul(B[i % 2][:, 0:G], wqkr[:, i, :], x2Tr[:, ds(g * G, G)],
                                  start=False, stop=True).then_inc(s_qk, 1)
                    if not first:
                        x3_turn(g - 1, NQK)
                    pe.wait_ge(s_qka, halves(g) + NQK // 2)
                    pe.wait_ge(s_qkd, halves(g) + NQK // 2)
                    pe.wait_ge(s_vin, g * 16 + 16)
                    scores(g, 0)
                    scores(g, 1)
                    for b in range(NB + 1):
                        if b + 2 < NB:
                            scores(g, b + 2)
                        if b < NB:
                            turn_probs(g, b)
                        if b >= 1:
                            weigh(g, b - 1)
                    pe.wait_ge(s_oa, g * NB + NB)
                    pe.wait_ge(s_od, g * NB + NB)
                    for t in range(NT):
                        for j in range(HEADS):
                            pe.matmul(tok_ps[:, t, :], om[:, t * T:(t + 1) * T, j], wpm[:, j, :],
                                      start=(j == 0), stop=False)
                            ins = pe.matmul(tok_ps[:, t, :], orr[:, t * T:(t + 1) * T, j], wpr[:, j, :],
                                            start=False, stop=(j == HEADS - 1))
                    ins.then_inc(s_proj, 1)

                pe.wait_ge(s_watt, 7 * 16)
                pe.wait_ge(s_blk, 1)
                group(0)
                with pe.Fori(1, NG) as g:
                    pe.wait_ge(s_hsum, g)
                    group(g)
                x3_turn(NG - 1, 0)

            def ring_item(eng, g, i, evac):
                eng.wait_ge(s_qk, items(g) + i + 1)
                m, r = (qm, qr) if i < NQK // 2 else (km, kr)
                p, w = (i % 12) // 3, i % 3
                wait(eng, s_e, g * NB)
                if w < 2:
                    return evac(m[:, :, 2 * p + w], B[i % 2][:, 0:G], bqks[:, i:i + 1])
                evac(r[:, :, 2 * p], B[i % 2][0:DR, 0:G], bqks[0:DR, i:i + 1])
                return evac(r[:, :, 2 * p + 1], B[i % 2][DR:128, 0:G], bqks[DR:128, i:i + 1])

            @block.scalar
            def _(act):
                def evac(o, i, bias):
                    return act.activation(o, i, ACT.Identity, bias=bias)

                def root(g):
                    act.wait_ge(s_var, g + 1)
                    act.activation(std[:, :], ve[:, :], ACT.Sqrt).then_inc(s_std, 1)

                def x3_main(g, at):
                    act.wait_ge(s_qk, items(g + 1) + at + 1)
                    act.activation(x3Tm[:, ds(g * G, G)], B[0][:, 0:G], ACT.Copy).then_inc(s_qka, 1)

                def group(g):
                    for i in range(0, NQK, 2):
                        ring_item(act, g, i, evac).then_inc(s_qka, 1)
                    if not isinstance(g, int):
                        x3_main(g - 1, NQK)
                    for s in range(NB + 2):
                        if s < NB:
                            act.wait_ge(s_sub, g * NB + s + 1)
                            act.activation(pr[:, s % 2, :, :], pr[:, s % 2, :, :], ACT.Exp).then_inc(s_exp, 1)
                        if 1 <= s <= NB:
                            b = s - 1
                            act.wait_ge(s_at, g * NB + b + 1)
                            if not isinstance(g, int) or b >= 2:
                                act.wait_ge(s_o, g * NB + b - 1)
                            act.activation(pt[:, b % 2, :], B[4 + b % 2][0:PAIR, 0:BW], ACT.Copy).then_inc(s_atsb, 1)
                        if s >= 2:
                            b = s - 2
                            act.wait_ge(s_o, g * NB + b + 1)
                            if not isinstance(g, int):
                                act.wait_ge(s_proj, g)
                            act.activation(om[:, b * 36:(b + 1) * 36, :].rearrange("p t j -> p (t j)"),
                                           B[6][:, 0:BW], ACT.Copy, scale=float(D) ** -0.5).then_inc(s_oa, 1)
                    root(g)

                group(0)
                with act.Fori(1, NG) as g:
                    group(g)
                x3_main(NG - 1, 0)

            @block.gpsimd
            def _(pool):
                with pool.Fori(0, NG) as g:
                    for b in range(NB):
                        pool.wait_ge(s_rec, g * NB + b + 1)
                        pool.tensor_tensor(pr[:, b % 2, :, :], pr[:, b % 2, :, :],
                                           ri[:, b % 2, :].unsqueeze(2).broadcast_to([PAIR, BP, PAIR]),
                                           ALU.mult).then_inc(s_prob, 1)

            @block.vector
            def _(dve):
                link = Chain(dve, s_dve)

                def evac(o, i, bias):
                    return dve.tensor_scalar(o, i, bias, None, ALU.add)

                def x3_rest(g, at):
                    dve.wait_ge(s_qk, items(g + 1) + at + 2)
                    dve.tensor_copy(x3Tr[:, ds(g * G, G)], B[1][0:DR, 0:G]).then_inc(s_qkd, 1)

                def group(g):
                    for i in range(1, NQK, 2):
                        ring_item(dve, g, i, evac).then_inc(s_qkd, 1)
                    if not isinstance(g, int):
                        x3_rest(g - 1, NQK)
                    for s in range(NB + 2):
                        if s < NB:
                            sc = B[2 + s % 2][0:PAIR, 0:BW].rearrange("p (n k) -> p n k", n=BP)
                            dve.wait_ge(s_e, g * NB + s + 1)
                            dve.tensor_reduce(mx[:, s % 2, :], sc, AX.X, ALU.max).then_inc(s_max, 1)
                            dve.wait_ge(s_max, g * NB + s + 1)
                            if not isinstance(g, int) or s >= 2:
                                dve.wait_ge(s_at, g * NB + s - 1)
                            dve.tensor_tensor(pr[:, s % 2, :, :], sc,
                                              mx[:, s % 2, :].unsqueeze(2).broadcast_to([PAIR, BP, PAIR]),
                                              ALU.subtract).then_inc(s_sub, 1)
                        if 1 <= s <= NB:
                            b = s - 1
                            dve.wait_ge(s_exp, g * NB + b + 1)
                            dve.tensor_reduce(sm[:, b % 2, :], pr[:, b % 2, :, :], AX.X, ALU.add).then_inc(s_sum, 1)
                            dve.wait_ge(s_sum, g * NB + b + 1)
                            if not isinstance(g, int) or b >= 2:
                                dve.wait_ge(s_prob, g * NB + b - 1)
                            dve.reciprocal(ri[:, b % 2, :], sm[:, b % 2, :]).then_inc(s_rec, 1)
                        if s >= 2:
                            b = s - 2
                            dve.wait_ge(s_o, g * NB + b + 1)
                            if not isinstance(g, int):
                                dve.wait_ge(s_proj, g)
                            dve.tensor_scalar(orr[:, b * 36:(b + 1) * 36, :].rearrange("p t j -> p (t j)"),
                                              B[7][0:DR, 0:BW], float(D) ** -0.5, None,
                                              ALU.mult).then_inc(s_od, 1)
                    link.loop(g, LN_LINKS + 1)
                    dve.wait_ge(s_proj, g + 1)
                    dve.tensor_tensor(hsum[:, :, :], tok_ps, bps[:, None, :].broadcast_to([T, NT, D]),
                                      ALU.add).then_inc(s_hsum, 1)
                    dve.wait_ge(s_hsum, g + 1)
                    hg = h_all[:, ds(g * NT, NT), :]
                    link(dve.tensor_tensor(hg, hg, hsum[:, :, :], ALU.add))

                    def xtok_free():
                        if not isinstance(g, int):
                            dve.wait_ge(s_qk, items(g) + RING)
                            dve.wait_ge(s_x3out, g * NT * 16)

                    layer_norm(dve, link, lambda t: h_all[:, ds(g * NT + t, 1), :].rearrange("p a d -> p (a d)"),
                               ln, g, s_var, s_std, xtok_free, s_xtok, spare)
                    link.end()

                dve.tensor_copy(blkb[:, :], blk[:, :]).then_inc(s_blk, 1)
                group(0)
                with dve.Fori(1, NG) as g:
                    group(g)
                x3_rest(NG - 1, 0)

        with ExitStack() as st:
            def sb(name, shape, dt=F32):
                return st.enter_context(nc.sbuf_tensor(name, shape, dt))

            def sem(name):
                return st.enter_context(nc.semaphore(name))

            gm = sb("gm", [DM, E])
            gr = sb("gr", [DR, E])
            wsm = sb("wsm", [DM, 2 * F_SH])
            wsr = sb("wsr", [DR, 2 * F_SH])
            wsd = sb("wsd", [128, KS, D])
            sgate = sb("sgate", [128, 2, G])
            sup = sb("sup", [128, 2, G])
            sa = sb("sa", [128, KS, G])
            ysh = sb("ysh", [T, NT, D])
            sc = sb("sc", [E, N])
            tops = sb("tops", [E, CAP])
            topi = sb("topi", [E, CAP], U32)
            topf = sb("topf", [E, CAP])
            idx = sb("idx", [HC, 2, E], U32)
            scr = sb("scr", [HC, 2, E])
            idc = sb("idc", [HC, 2, 2], U32)
            wgm = [sb(f"wgm{u}", [DM, 2 * F_EXP]) for u in range(2)]
            wgr = [sb(f"wgr{u}", [DR, 2 * F_EXP]) for u in range(2)]
            wd = [sb(f"wd{u}", [128, KF, D]) for u in range(2)]
            xg = [sb(f"xg{u}", [HC, 2, D]) for u in range(2)]
            xgm = [sb(f"xgm{u}", [DM, CAP]) for u in range(2)]
            xgr = [sb(f"xgr{u}", [DR, CAP]) for u in range(2)]
            sl = sb("sl", [128, 2, 2, CAP])
            aT = [sb(f"aT{u}", [128, KF, CAP]) for u in range(2)]
            ys = [sb(f"ys{u}", [HC, 2, D]) for u in range(2)]

            s_ws = sem("s_ws")
            s_rps = sem("s_rps")
            s_sc = sem("s_sc")
            s_top = sem("s_top")
            s_topT = sem("s_topT")
            s_idx = sem("s_idx")
            s_sg = sem("s_sg")
            s_sga = sem("s_sga")
            s_sa = sem("s_sa")
            s_sd = sem("s_sd")
            s_sda = sem("s_sda")
            s_ysh = sem("s_ysh")
            s_init = sem("s_init")
            s_we = [sem(f"s_we{u}") for u in range(2)]
            s_idc = sem("s_idc")
            s_gath = [sem(f"s_gath{u}") for u in range(2)]
            s_xgt = sem("s_xgt")
            s_xga = sem("s_xga")
            s_xgd = sem("s_xgd")
            s_gu = sem("s_gu")
            s_silu = sem("s_silu")
            s_act = sem("s_act")
            s_y = sem("s_y")
            s_ys = sem("s_ys")
            s_scat = sem("s_scat")
            s_carry = sem("s_carry")
            block = st.enter_context(nc.Block())

            ITEMS = KF // 2

            @block.sync
            def _(sp):
                sp.dma_start(gm[:, :], gateT[0:DM, :]).then_inc(s_ws, 16)
                sp.dma_start(gr[:, :], gateT[DM:D, :]).then_inc(s_ws, 16)
                sp.dma_start(wsm[:, :], Wsgu[0:DM, :]).then_inc(s_ws, 16)
                sp.dma_start(wsr[:, :], Wsgu[DM:D, :]).then_inc(s_ws, 16)
                sp.dma_start(wsd[:, :, :], Wsd).then_inc(s_ws, 16)

                def load(e, u):
                    sp.dma_start(wgm[u][:, :], Wgu[ds(e, 1), 0:DM, :].rearrange("a p f -> (a p) f")).then_inc(s_we[u], 16)
                    sp.dma_start(wgr[u][:, :], Wgu[ds(e, 1), DM:D, :].rearrange("a p f -> (a p) f")).then_inc(s_we[u], 16)
                    sp.dma_start(wd[u][:, :, :], Wd[ds(e, 1)].rearrange("a p k d -> (a p) k d")).then_inc(s_we[u], 16)

                load(0, 0)
                load(1, 1)
                with sp.Fori(0, NG) as g:
                    sp.wait_ge(s_ysh, g + 1)
                    for t in range(NT):
                        sp.dma_start(out_rows[ds(g * G + t * T, T), :], ysh[:, t, :]).then_inc(s_init, 16)
                with sp.Fori(1, E // 2) as i:
                    for u in range(2):
                        sp.wait_ge(s_y, 2 * i + u - 1)
                        load(2 * i + u, u)

            @block.tensor
            def _(pe):
                pe.wait_ge(s_ws, 5 * 16)
                for c in range(3):
                    cs = slice(c * 384, (c + 1) * 384)
                    pe.matmul(B[5 + c][0:E, 0:384], gm[:, :], x3Tm[:, cs], start=True, stop=False)
                    ins = pe.matmul(B[5 + c][0:E, 0:384], gr[:, :], x3Tr[:, cs], start=False, stop=True)
                ins.then_inc(s_rps, 1)
                def shared(g):
                    xm, xr = x3Tm[:, ds(g * G, G)], x3Tr[:, ds(g * G, G)]
                    for m in range(KS):
                        wait(pe, s_sga, g * KS + m)
                        for w in range(2):
                            o = B[w][:, 0:G]
                            fs = slice(w * F_SH + m * 128, w * F_SH + (m + 1) * 128)
                            pe.matmul(o, wsm[:, fs], xm, start=True, stop=False)
                            ins = pe.matmul(o, wsr[:, fs], xr, start=False, stop=True)
                        ins.then_inc(s_sg, 1)
                    pe.wait_ge(s_sa, g * KS + KS)
                    wait(pe, s_sda, g * NT)
                    for t in range(NT):
                        for k in range(KS):
                            ins = pe.matmul(B[2 + t][0:T, 0:D], sa[:, k, t * T:(t + 1) * T], wsd[:, k, :],
                                            start=(k == 0), stop=(k == KS - 1))
                    ins.then_inc(s_sd, 1)

                shared(0)
                with pe.Fori(1, NG) as g:
                    shared(g)
                pe.wait_ge(s_top, 3 * ROUNDS + 1)
                pe.wait_ge(s_sc, 3)
                for n in range(2):
                    for h in range(2):
                        src = (topf, tops)[n]
                        ins = pe.transpose(B[5][0:HC, (2 * n + h) * E:(2 * n + h + 1) * E],
                                           src[:, h * HC:(h + 1) * HC], ident[0:E, 0:E])
                ins.then_inc(s_topT, 1)
                pe.wait_ge(s_idx, 2)

                def expert(i, u):
                    e = 2 * i + u
                    pe.wait_ge(s_gath[u], 32 * i + 32)
                    wait(pe, s_xga, e)
                    wait(pe, s_xgd, e)
                    for h in range(2):
                        pe.transpose(B[5][:, h * HC:(h + 1) * HC], xg[u][:, h, 0:DM], ident[0:HC, 0:HC])
                        ins = pe.transpose(B[4][0:DR, h * HC:(h + 1) * HC], xg[u][:, h, DM:D],
                                           ident[0:HC, 0:HC])
                    ins.then_inc(s_xgt, 1)
                    pe.wait_ge(s_xga, e + 1)
                    pe.wait_ge(s_xgd, e + 1)
                    pe.wait_ge(s_we[u], 48 * i + 48)
                    for n in range(ITEMS):
                        r = (ITEMS * u + n) % 2
                        wait(pe, s_act, e * ITEMS + (n - 1 if n else 0))
                        for w in range(2):
                            for m in range(2):
                                o = B[2 * w + r][:, m * CAP:(m + 1) * CAP]
                                f = w * F_EXP + (2 * n + m) * 128
                                pe.matmul(o, wgm[u][:, f:f + 128], xgm[u][:, :], start=True, stop=False)
                                ins = pe.matmul(o, wgr[u][:, f:f + 128], xgr[u][:, :], start=False, stop=True)
                        ins.then_inc(s_gu, 1)
                    pe.wait_ge(s_act, e * ITEMS + ITEMS)
                    pe.wait_ge(s_ys, 2 * e - 2) if not isinstance(e, int) or e >= 2 else None
                    for h in range(2):
                        for k in range(KF):
                            ins = pe.matmul(B[6 + u][0:HC, h * 256:h * 256 + D], aT[u][:, k, h * HC:(h + 1) * HC],
                                            wd[u][:, k, :], start=(k == 0), stop=(k == KF - 1))
                    ins.then_inc(s_y, 1)

                expert(0, 0)
                expert(0, 1)
                with pe.Fori(1, E // 2) as i:
                    expert(i, 0)
                    expert(i, 1)

            @block.scalar
            def _(act):
                act.wait_ge(s_rps, 1)
                for c in range(3):
                    act.activation(sc[:, c * 384:(c + 1) * 384], B[5 + c][0:E, 0:384], ACT.Sigmoid).then_inc(s_sc, 1)
                def shared(g):
                    for m in range(KS):
                        i = g * KS + m
                        act.wait_ge(s_sg, i + 1)
                        wait(act, s_sa, i)
                        act.activation(sgate[:, 0, :], B[0][:, 0:G], ACT.Silu)
                        act.activation(sup[:, 0, :], B[1][:, 0:G], ACT.Copy).then_inc(s_sga, 1)
                    act.wait_ge(s_sd, g + 1)
                    wait(act, s_init, g * NT * 16)
                    wait(act, s_ysh, g)
                    for t in range(NT):
                        act.activation(ysh[:, t, :], B[2 + t][0:T, 0:D], ACT.Copy).then_inc(s_sda, 1)

                shared(0)
                with act.Fori(1, NG) as g:
                    shared(g)

                def expert(i, u):
                    e = 2 * i + u
                    act.wait_ge(s_xgt, e + 1)
                    act.activation(xgm[u][:, :], B[5][:, 0:CAP], ACT.Copy).then_inc(s_xga, 1)
                    for n in range(ITEMS):
                        r = (ITEMS * u + n) % 2
                        act.wait_ge(s_gu, e * ITEMS + n + 1)
                        act.activation(sl[:, r, :, :], B[r][:, 0:2 * CAP].rearrange("p (m c) -> p m c", m=2),
                                       ACT.Silu).then_inc(s_silu, 1)

                with act.Fori(0, E // 2) as i:
                    expert(i, 0)
                    expert(i, 1)

            @block.gpsimd
            def _(pool):
                def shared(g):
                    for m in range(KS):
                        pool.wait_ge(s_sga, g * KS + m + 1)
                        wait(pool, s_sd, g)
                        pool.tensor_tensor(sa[:, m, :], sgate[:, 0, :], sup[:, 0, :], ALU.mult).then_inc(s_sa, 1)
                    pool.wait_ge(s_sda, g * NT + NT)
                    pool.tensor_tensor(ysh[:, :, :], ysh[:, :, :], h_all[:, ds(g * NT, NT), :],
                                       ALU.add).then_inc(s_ysh, 1)

                shared(0)
                with pool.Fori(1, NG) as g:
                    shared(g)
                pool.wait_ge(s_idx, 2)

                def carry_wait(n):
                    wait(pool, s_carry, n)
                    pool.tensor_tensor(pspare[:, 0:1], pspare[:, 1:2], pspare[:, 1:2], ALU.mult).then_inc(s_carry, 1)

                def gather(e, i, u):
                    pool.wait_ge(s_xgt, e - 1) if not isinstance(e, int) or e >= 2 else None
                    pool.tensor_copy(idc[:, u, :], idx[:, :, ds(e, 1)].rearrange("p h a -> p (h a)")).then_inc(s_idc, 1)
                    pool.wait_ge(s_idc, e + 1)
                    carry_wait(2 * e - 1)
                    for h in range(2):
                        pool.indirect_dma_start(xg[u][:, h, :], None, x3_dram,
                                                bass.IndirectOffsetOnAxis(ap=idc[:, u, h:h + 1], axis=0)
                                                ).then_inc(s_gath[u], 16)

                def scatter(e, u, n):
                    pool.wait_ge(s_ys, 2 * e + 2)
                    wait(pool, s_scat, e * 32)
                    carry_wait(n)
                    for h in range(2):
                        pool.indirect_dma_start(out_rows, bass.IndirectOffsetOnAxis(ap=idc[:, u, h:h + 1], axis=0),
                                                ys[u][:, h, :], None, compute_op=ALU.add).then_inc(s_scat, 16)

                pool.wait_ge(s_init, NG * NT * 16)
                gather(0, 0, 0)
                gather(1, 0, 1)

                def turn(i):
                    for u in range(2):
                        scatter(2 * i + u, u, 4 * i + 2 * u + 2)
                        pool.wait_ge(s_scat, (2 * i + u) * 32 + 32)
                        gather(2 * i + 2 + u, i + 1, u)

                turn(0)
                with pool.Fori(1, E // 2 - 1) as i:
                    turn(i)
                scatter(E - 2, 0, 2 * E - 2)
                scatter(E - 1, 1, 2 * E - 1)
                pool.wait_ge(s_scat, E * 32)

            @block.vector
            def _(dve):
                dve.wait_ge(s_sc, 3)
                for r in range(ROUNDS):
                    rs8 = slice(8 * r, 8 * r + 8)
                    dve.max(tops[:, rs8], sc[:, :]).then_inc(s_top, 1)
                    dve.wait_ge(s_top, 3 * r + 1)
                    dve.max_index(topi[:, rs8], tops[:, rs8], sc[:, :]).then_inc(s_top, 1)
                    dve.wait_ge(s_top, 3 * r + 2)
                    dve.match_replace(sc[:, :], tops[:, rs8], sc[:, :], -1.0).then_inc(s_top, 1)
                    dve.wait_ge(s_top, 3 * r + 3)
                dve.tensor_copy(topf[:, :], topi[:, :]).then_inc(s_top, 1)
                dve.wait_ge(s_topT, 1)
                dve.tensor_copy(idx[:, :, :], B[5][0:HC, 0:2 * E].rearrange("p (h e) -> p h e", h=2)).then_inc(s_idx, 1)
                dve.tensor_copy(scr[:, :, :], B[5][0:HC, 2 * E:4 * E].rearrange("p (h e) -> p h e", h=2)).then_inc(s_idx, 1)
                dve.wait_ge(s_idx, 2)

                def expert(i, u):
                    e = 2 * i + u
                    dve.wait_ge(s_xgt, e + 1)
                    dve.tensor_copy(xgr[u][:, :], B[4][0:DR, 0:CAP]).then_inc(s_xgd, 1)
                    for n in range(ITEMS):
                        r = (ITEMS * u + n) % 2
                        dve.wait_ge(s_silu, e * ITEMS + n + 1)
                        dve.tensor_tensor(aT[u][:, 2 * n:2 * n + 2, :],
                                          B[2 + r][:, 0:2 * CAP].rearrange("p (m c) -> p m c", m=2),
                                          sl[:, r, :, :], ALU.mult).then_inc(s_act, 1)
                    dve.wait_ge(s_y, e + 1)
                    dve.wait_ge(s_scat, 32 * (e - 1)) if not isinstance(e, int) or e >= 2 else None
                    for h in range(2):
                        dve.tensor_scalar(ys[u][:, h, :], B[6 + u][0:HC, h * 256:h * 256 + D],
                                          scr[:, h, ds(e, 1)], None, ALU.mult).then_inc(s_ys, 1)

                expert(0, 0)
                expert(0, 1)
                with dve.Fori(1, E // 2) as i:
                    expert(i, 0)
                    expert(i, 1)


def kernel(**inputs):
    import numpy as _np
    import concourse.bacc as _bacc
    from concourse import mybir as _mybir
    from concourse.bass_utils import run_bass_kernel_spmd as _run

    a = {k: _np.asarray(v) for k, v in inputs.items()}
    x = a["x"].reshape(IMAGES, 3, 6, PATCH, 6, PATCH).transpose(0, 2, 4, 1, 3, 5).reshape(NG, G, KI, 128)
    Wq, Wk, Wv = _np.split(a["L0_attn_W_qkv"], 3, axis=1)
    bq, bk, bv = _np.split(a["L0_attn_b_qkv"], 3)

    def tiles(w):
        w = w.reshape(-1, 4, 2, D)
        rest = w[:, :, :, DM:].reshape(-1, 4, 1, 128)
        return _np.concatenate([w[:, :, :, :DM], rest], axis=2).reshape(-1, 12, 128)

    rows = _np.arange(PAIR) < PAIR // 2
    blocks = _np.zeros((2, 2 * PAIR), _np.float32)
    blocks[0, :PAIR], blocks[1, :PAIR] = rows, ~rows
    blocks[0, PAIR:], blocks[1, PAIR:] = _np.where(~rows, -1e30, 0), _np.where(rows, -1e30, 0)
    arrays = {
        "xT": x.transpose(0, 3, 2, 1),
        "W1": a["L0_tok_W1"].reshape(KI, 128, KH, 128).transpose(2, 1, 0, 3),
        "b1": a["L0_tok_b1"].reshape(KH, 128).T,
        "W2": a["L0_tok_W2"].reshape(KH, 128, D).transpose(1, 0, 2),
        "b2": a["L0_tok_b2"],
        "Wqk": _np.concatenate([tiles(Wq), tiles(Wk)], axis=1),
        "bqk": _np.concatenate([tiles(bq), tiles(bk)], axis=1)[0].T,
        "Wv": Wv, "bv": bv,
        "Wp": a["L0_attn_W_proj"].reshape(HEADS, D, D).transpose(1, 0, 2),
        "bp": a["L0_attn_b_proj"],
        "blocks": blocks,
        "gateT": a["L0_ffn_gate_weight"].T,
        "Wgu": _np.concatenate([a["L0_ffn_Wg"].transpose(0, 2, 1), a["L0_ffn_Wu"].transpose(0, 2, 1)], axis=2),
        "Wd": a["L0_ffn_Wd"].transpose(0, 2, 1).reshape(E, KF, 128, D).transpose(0, 2, 1, 3),
        "Wsgu": _np.concatenate([a["L0_ffn_Ws_g"].T, a["L0_ffn_Ws_u"].T], axis=1),
        "Wsd": a["L0_ffn_Ws_d"].T.reshape(KS, 128, D).transpose(1, 0, 2),
    }
    nc = _bacc.Bacc("TRN2", target_bir_lowering=False, num_devices=1)
    feed, args = {}, []
    for name, v in arrays.items():
        v = _np.ascontiguousarray(v)
        feed[f"in_{name}"] = v
        args.append(nc.dram_tensor(f"in_{name}", v.shape, _mybir.dt.from_np(v.dtype), kind="ExternalInput").ap())
    args.append(nc.dram_tensor("out_0", (IMAGES, SEQ, D), _mybir.dt.float32, kind="ExternalOutput").ap())
    vit_moe_kernel(nc, *args)
    r = _run(nc, [feed], core_ids=[0])
    return r.results[0]["out_0"]
```

```python
from contextlib import ExitStack

import concourse.bass as bass
import concourse.mybir as mybir

F32 = mybir.dt.float32
BF16 = mybir.dt.bfloat16
U32 = mybir.dt.uint32
ACT = mybir.ActivationFunctionType
ALU = mybir.AluOpType
AX = mybir.AxisListType

IMAGES, SEQ, D = 32, 36, 192
N = IMAGES * SEQ
PATCH = 16
IN_DIM = 3 * PATCH * PATCH
HID = 768
HEADS = 8
QKV = HEADS * D
E, F_EXP, TOP_K, F_SH = 16, 768, 2, 384
CAP = N * TOP_K // E
EPS = 1e-5

G = 288
NG = N // G
T = 96
NT = G // T
KI = IN_DIM // 128
KH = HID // 128
DM, DR = 128, D - 128
PAIR = 72
BP = 4
NB = G // 9 // BP
BW = BP * PAIR
NQK = 24
HC = CAP // 2
KF = F_EXP // 128
KS = F_SH // 128
ROUNDS = CAP // 8
LN_LINKS = 13
ds = bass.ds


def wait(eng, sem, value):
    if not isinstance(value, int) or value > 0:
        eng.wait_ge(sem, value)


class Chain:

    def __init__(self, eng, sem, start=0):
        self.eng, self.sem, self.n, self.off = eng, sem, start, 0

    def __call__(self, ins):
        self.n += 1
        ins.then_inc(self.sem, 1)
        self.eng.wait_ge(self.sem, self.off + self.n)

    def loop(self, turn, per):
        self.n, self.per, self.off = 0, per, turn * per

    def end(self):
        assert self.n == self.per, (self.n, self.per)


def layer_norm(dve, link, src, ln, turn, s_var, s_std, xtok_free, s_xtok, spare):
    dve.memset(spare, 0.0)
    for t in range(NT):
        dve.bn_stats(ln["stats"][:, t, :], src(t)).then_inc(ln["s_stat"], 1)
    dve.wait_ge(ln["s_stat"], turn * NT + NT)
    dve.memset(spare, 0.0)
    for t in range(NT - 1):
        dve.bn_aggr(ln["mv"][:, t, :], ln["stats"][:, t, :])
    link(dve.bn_aggr(ln["mv"][:, NT - 1, :], ln["stats"][:, NT - 1, :]))
    ve, std, rs, rt = ln["ve"], ln["std"], ln["rs"], ln["rt"]
    dve.tensor_scalar(ve[:, :], ln["mv"][:, :, 1], EPS, None, ALU.add).then_inc(s_var, 1)
    dve.wait_ge(s_std, turn + 1)
    link(dve.reciprocal(rs[:, :], std[:, :]))
    link(dve.tensor_tensor(rt[:, :], rs[:, :], rs[:, :], ALU.mult))
    link(dve.tensor_tensor(rt[:, :], rt[:, :], ve[:, :], ALU.mult))
    link(dve.tensor_scalar(rt[:, :], rt[:, :], -0.5, 1.5, ALU.mult, ALU.add))
    link(dve.tensor_tensor(rs[:, :], rs[:, :], rt[:, :], ALU.mult))
    xtok_free()
    for t in range(NT):
        ins = dve.tensor_scalar(ln["xtok"][:, t, :], src(t), ln["mv"][:, t, 0:1], rs[:, t:t + 1],
                                ALU.subtract, ALU.mult)
        ins.then_inc(s_xtok, 1)


LN_LINKS = 6

OWNER = "AAAAAAAADADDADDADDADDADD" + "AD"
RING = len(OWNER)
RING_BANKS = [0, 1, 4, 5]
SCORE_BANKS = [2, 3, 0, 1]
AHEAD = 3


def owned(who, i):
    return OWNER[:i].count(who)


def vit_moe_kernel(nc, xT, W1, b1, W2, b2, Wqk, bqk, Wv, bv, Wp, bp, blocks, gateT, Wgu, Wd, Wsgu, Wsd, out):
    with ExitStack() as ctx:
        def sb(name, shape, dt=F32):
            return ctx.enter_context(nc.sbuf_tensor(name, shape, dt))

        def sem(name):
            return ctx.enter_context(nc.semaphore(name))

        out_rows = out.rearrange("a b c -> (a b) c")
        v_dram = nc.dram_tensor("v_scratch", [N, QKV], F32, kind="Internal").ap()
        x3_dram = nc.dram_tensor("x3_scratch", [N, D], F32, kind="Internal").ap()

        ident = sb("ident", [128, 128])
        h_all = sb("h_all", [T, NG * NT, D])
        x2Tm = sb("x2Tm", [DM, N])
        x2Tr = sb("x2Tr", [DR, N])
        x3Tm = sb("x3Tm", [DM, N])
        x3Tr = sb("x3Tr", [DR, N])
        hsum = sb("hsum", [T, NT, D])
        spare = sb("spare", [1, 1])[:, :]
        pspare = sb("pspare", [1, 2])
        ln = {"stats": sb("stats", [T, NT, 6]), "mv": sb("mv", [T, NT, 2]), "ve": sb("ve", [T, NT]),
              "std": sb("std", [T, NT]), "rs": sb("rs", [T, NT]), "rt": sb("rt", [T, NT]),
              "xtok": sb("xtok", [T, NT, D])}
        xtok, ve, std = ln["xtok"], ln["ve"], ln["std"]

        wqkm = sb("wqkm", [DM, NQK, 128])
        wqkr = sb("wqkr", [DR, NQK, 128])
        bqks = sb("bqks", [128, NQK])
        wpm = sb("wpm", [DM, HEADS, D])
        wpr = sb("wpr", [DR, HEADS, D])
        bps = sb("bps", [T, D])
        blk = sb("blk", [2, 2 * PAIR])

        B = [ctx.enter_context(nc.psum_tensor(f"bank{i}", [128, 512], F32)) for i in range(6)]
        ps67 = ctx.enter_context(nc.psum_tensor("bank67", [128, 1024], F32))
        B += [ps67[:, 0:512], ps67[:, 512:1024]]
        tok_ps = ps67[0:T, 0:NT * 256].rearrange("p (t c) -> p t c", t=NT)[:, :, 0:D]

        s_watt = sem("s_watt")

        with ExitStack() as st:
            def sb(name, shape, dt=F32):
                return st.enter_context(nc.sbuf_tensor(name, shape, dt))

            def sem(name):
                return st.enter_context(nc.semaphore(name))

            xs = sb("xs", [128, NG, KI, G])
            w1 = sb("w1", [128, KH, KI, 128])
            w2 = sb("w2", [128, KH, D])
            b1s = sb("b1s", [128, KH])
            b2s = sb("b2s", [T, D])
            wvm = sb("wvm", [DM, QKV])
            wvr = sb("wvr", [DR, QKV])
            bvs = sb("bvs", [T, QKV])
            hT = sb("hT", [128, KH, G])
            x2gm = sb("x2gm", [DM, G])
            x2gr = sb("x2gr", [DR, G])
            vtok = sb("vtok", [T, NT, QKV])

            s_id = sem("s_id")
            s_x = [sem(f"s_x{g}") for g in range(NG)]
            s_w1 = [sem(f"s_w1_{m}") for m in range(KH)]
            s_small = sem("s_small")
            s_w2v = sem("s_w2v")
            s_tok1 = sem("s_tok1")
            s_hT = sem("s_hT")
            s_tok2 = sem("s_tok2")
            s_hsum = sem("s_hsum")
            s_var = sem("s_var")
            s_std = sem("s_std")
            s_xtok = sem("s_xtok")
            s_x2ps = sem("s_x2ps")
            s_x2a = sem("s_x2a")
            s_x2d = sem("s_x2d")
            s_v = sem("s_v")
            s_vsb = sem("s_vsb")
            s_vout = [sem(f"s_vout{t}") for t in range(NT)]
            s_dve = sem("s_dve")
            ln["s_stat"] = sem("s_stat")
            block = st.enter_context(nc.Block())

            @block.sync
            def _(sp):
                for g in range(NG):
                    sp.dma_start(xs[:, g, :, :], xT[g]).then_inc(s_x[g], 16)
                    if g == 0:
                        for m in range(KH):
                            sp.dma_start(w1[:, m, :, :], W1[m]).then_inc(s_w1[m], 16)
                        sp.dma_start(b1s[:, :], b1).then_inc(s_small, 16)
                        sp.dma_start(b2s[:, :], b2.partition_broadcast(T)).then_inc(s_small, 16)
                        sp.dma_start(bvs[:, :], bv.partition_broadcast(T)).then_inc(s_small, 16)
                        sp.dma_start(w2[:, :, :], W2).then_inc(s_w2v, 16)
                        sp.dma_start(wvm[:, :], Wv[0:DM, :]).then_inc(s_w2v, 16)
                        sp.dma_start(wvr[:, :], Wv[DM:D, :]).then_inc(s_w2v, 16)
                sp.dma_start(wqkm[:, :, :], Wqk[0:DM]).then_inc(s_watt, 16)
                sp.dma_start(wqkr[:, :, :], Wqk[DM:D]).then_inc(s_watt, 16)
                sp.dma_start(bqks[:, :], bqk).then_inc(s_watt, 16)
                sp.dma_start(wpm[:, :, :], Wp[0:DM]).then_inc(s_watt, 16)
                sp.dma_start(wpr[:, :, :], Wp[DM:D]).then_inc(s_watt, 16)
                sp.dma_start(bps[:, :], bp.partition_broadcast(T)).then_inc(s_watt, 16)
                sp.dma_start(blk[:, :], blocks).then_inc(s_watt, 16)
                with sp.Fori(0, NG) as g:
                    for t in range(NT):
                        sp.wait_ge(s_vsb, g * 9 + 3 * t + 3)
                        sp.dma_start(v_dram[ds(g * G + t * T, T), :], vtok[:, t, :]).then_inc(s_vout[t], 16)
                for t in range(NT):
                    sp.wait_ge(s_vout[t], 16 * NG)
                sp.wait_ge(s_watt, 7 * 16)

            @block.gpsimd
            def _(pool):
                pool.memset(pspare[:, :], 0.0)
                pool.memset(ident[:, :], 0.0).then_inc(s_id, 1)
                pool.wait_ge(s_id, 1)
                pool.affine_select(out=ident[:, :], in_=ident[:, :], compare_op=ALU.not_equal, fill=1.0, base=0,
                                   pattern=[[-1, 128]], channel_multiplier=1).then_inc(s_id, 1)

            @block.tensor
            def _(pe):
                def tok1(g):
                    for m in range(KH):
                        if isinstance(g, int) and g == 0:
                            pe.wait_ge(s_w1[m], 16)
                        wait(pe, s_hT, g * KH + m - 1)
                        for k in range(KI):
                            x = xs[:, ds(g, 1), k, :].rearrange("p a b -> p (a b)")
                            ins = pe.matmul(B[m % 2][:, 0:G], w1[:, m, k, :], x, start=(k == 0), stop=(k == KI - 1))
                        ins.then_inc(s_tok1, 1)

                def tok2(g):
                    pe.wait_ge(s_hT, g * KH + KH)
                    wait(pe, s_hsum, g)
                    for t in range(NT):
                        for k in range(KH):
                            ins = pe.matmul(tok_ps[:, t, :], hT[:, k, t * T:(t + 1) * T], w2[:, k, :],
                                            start=(k == 0), stop=(k == KH - 1))
                    ins.then_inc(s_tok2, 1)

                def turn_and_v(g):
                    pe.wait_ge(s_xtok, g * NT + NT)
                    wait(pe, s_x2a, g * 2)
                    wait(pe, s_x2d, g * 2)
                    for t in range(NT):
                        pe.transpose(B[2][:, t * T:(t + 1) * T], xtok[:, t, 0:DM], ident[0:T, 0:T])
                    for t in range(NT):
                        ins = pe.transpose(B[3][0:DR, t * T:(t + 1) * T], xtok[:, t, DM:D], ident[0:T, 0:T])
                    ins.then_inc(s_x2ps, 1)
                    pe.wait_ge(s_x2a, g * 2 + 1)
                    pe.wait_ge(s_x2d, g * 2 + 1)
                    for t in range(NT):
                        for c in range(3):
                            i = 3 * t + c
                            wait(pe, s_vsb, g * 9 + (i - 1 if i else 0))
                            o = B[4 + i % 2][0:T, :]
                            cs = slice(c * 512, (c + 1) * 512)
                            pe.matmul(o, x2gm[:, t * T:(t + 1) * T], wvm[:, cs], start=True, stop=False)
                            pe.matmul(o, x2gr[:, t * T:(t + 1) * T], wvr[:, cs],
                                      start=False, stop=True).then_inc(s_v, 1)

                pe.wait_ge(s_x[0], 16)
                tok1(0)
                pe.wait_ge(s_w2v, 48)
                pe.wait_ge(s_id, 2)
                for g in range(1, NG):
                    pe.wait_ge(s_x[g], 16)
                tok2(0)
                tok1(1)
                turn_and_v(0)
                with pe.Fori(1, NG - 1) as g:
                    tok2(g)
                    tok1(g + 1)
                    turn_and_v(g)
                tok2(NG - 1)
                turn_and_v(NG - 1)

            @block.scalar
            def _(act):
                def hidden(g, m):
                    act.wait_ge(s_tok1, g * KH + m + 1)
                    act.activation(hT[:, m, :], B[m % 2][:, 0:G], ACT.Relu, bias=b1s[:, m:m + 1]).then_inc(s_hT, 1)

                def root(g):
                    act.wait_ge(s_var, g + 1)
                    act.activation(std[:, :], ve[:, :], ACT.Sqrt).then_inc(s_std, 1)

                def turned(g):
                    act.wait_ge(s_x2ps, g + 1)
                    act.activation(x2gm[:, :], B[2][:, 0:G], ACT.Copy).then_inc(s_x2a, 1)
                    act.activation(x2Tm[:, ds(g * G, G)], B[2][:, 0:G], ACT.Copy).then_inc(s_x2a, 1)

                act.wait_ge(s_small, 48)
                for m in range(KH):
                    hidden(0, m)
                with act.Fori(0, NG - 1) as g:
                    hidden(g + 1, 0)
                    root(g)
                    for m in range(1, KH):
                        hidden(g + 1, m)
                    turned(g)
                root(NG - 1)
                turned(NG - 1)

            @block.vector
            def _(dve):
                link = Chain(dve, s_dve)
                dve.wait_ge(s_small, 48)

                def group(g):
                    link.loop(g, LN_LINKS + 1)
                    dve.wait_ge(s_tok2, g + 1)
                    dve.tensor_tensor(hsum[:, :, :], tok_ps, b2s[:, None, :].broadcast_to([T, NT, D]),
                                      ALU.add).then_inc(s_hsum, 1)
                    dve.wait_ge(s_hsum, g + 1)
                    link(dve.tensor_scalar(h_all[:, ds(g * NT, NT), :], hsum[:, :, :], 0.0, None, ALU.max))

                    def xtok_free():
                        wait(dve, s_x2ps, g)

                    layer_norm(dve, link, lambda t: h_all[:, ds(g * NT + t, 1), :].rearrange("p a d -> p (a d)"),
                               ln, g, s_var, s_std, xtok_free, s_xtok, spare)
                    dve.wait_ge(s_x2ps, g + 1)
                    dve.tensor_copy(x2gr[:, :], B[3][0:DR, 0:G]).then_inc(s_x2d, 1)
                    dve.tensor_copy(x2Tr[:, ds(g * G, G)], B[3][0:DR, 0:G]).then_inc(s_x2d, 1)
                    for t in range(NT):
                        wait(dve, s_vout[t], g * 16)
                        for c in range(3):
                            i = 3 * t + c
                            cs = slice(c * 512, (c + 1) * 512)
                            dve.wait_ge(s_v, g * 9 + i + 1)
                            dve.tensor_tensor(vtok[:, t, cs], B[4 + i % 2][0:T, :], bvs[:, cs],
                                              ALU.add).then_inc(s_vsb, 1)
                    link.end()

                group(0)
                with dve.Fori(1, NG) as g:
                    group(g)

        with ExitStack() as st:
            def sb(name, shape, dt=F32):
                return st.enter_context(nc.sbuf_tensor(name, shape, dt))

            def sem(name):
                return st.enter_context(nc.semaphore(name))

            qm = sb("qm", [DM, G, HEADS])
            qr = sb("qr", [DR, G, HEADS])
            km = sb("km", [DM, G, HEADS])
            kr = sb("kr", [DR, G, HEADS])
            vp = sb("vp", [PAIR, NB * BP, D])
            om = sb("om", [DM, G, HEADS])
            orr = sb("orr", [DR, G, HEADS])
            pr = sb("pr", [PAIR, 4, BP, PAIR])
            pt = sb("pt", [PAIR, 2, BW])
            mx = sb("mx", [PAIR, 4, BP])
            sm = sb("sm", [PAIR, 4, BP])
            ri = sb("ri", [PAIR, 4, BP])
            blkb = sb("blkb", [2, 2 * PAIR], BF16)

            s_blk = sem("s_blk")
            s_qk = sem("s_qk")
            s_qka = sem("s_qka")
            s_qkd = sem("s_qkd")
            s_vin = sem("s_vin")
            s_e = sem("s_e")
            s_max = sem("s_max")
            s_sub = sem("s_sub")
            s_exp = sem("s_exp")
            s_sum = sem("s_sum")
            s_rec = sem("s_rec")
            s_prob = sem("s_prob")
            s_at = sem("s_at")
            s_atsb = sem("s_atsb")
            s_o = sem("s_o")
            s_oa = sem("s_oa")
            s_proj = sem("s_proj")
            s_hsum = sem("s_hsum2")
            s_var = sem("s_var2")
            s_std = sem("s_std2")
            s_xtok = sem("s_xtok2")
            s_x3out = sem("s_x3out")
            s_dve = sem("s_dve2")
            ln["s_stat"] = sem("s_stat2")
            block = st.enter_context(nc.Block())


            def items(g):
                return g * RING - 2 if not isinstance(g, int) or g > 0 else 0

            def evacuated(who, g, i):
                before = g * owned(who, RING) - 1 if not isinstance(g, int) or g > 0 else 0
                return before + owned(who, i)

            def bank(i):
                return B[RING_BANKS[i % 4]]

            @block.sync
            def _(sp):

                def group(g):
                    wait(sp, s_o, g * NB)
                    sp.dma_start(vp[:, :, :], v_dram[ds(g * G, G), :].rearrange(
                        "(n t) (j d) -> (t j) n d", t=9, j=HEADS)).then_inc(s_vin, 16)
                    sp.wait_ge(s_xtok, g * NT + NT)
                    for t in range(NT):
                        sp.dma_start(x3_dram[ds(g * G + t * T, T), :], xtok[:, t, :]).then_inc(s_x3out, 16)

                group(0)
                with sp.Fori(1, NG) as g:
                    group(g)
                sp.wait_ge(s_x3out, 16 * NT * NG)

            @block.tensor
            def _(pe):
                def ring_free(g, i):
                    if i >= 4:
                        who = OWNER[i - 4]
                        pe.wait_ge(s_qka if who == "A" else s_qkd, evacuated(who, g, i - 3))

                def x3_turn(g, at):
                    pe.wait_ge(s_xtok, g * NT + NT)
                    ring_free(g + 1, at)
                    ring_free(g + 1, at + 1)
                    for t in range(NT):
                        ins = pe.transpose(bank(at)[:, t * T:(t + 1) * T], xtok[:, t, 0:DM], ident[0:T, 0:T])
                    ins.then_inc(s_qk, 1)
                    for t in range(NT):
                        ins = pe.transpose(bank(at + 1)[0:DR, t * T:(t + 1) * T], xtok[:, t, DM:D], ident[0:T, 0:T])
                    ins.then_inc(s_qk, 1)

                def scores(g, b):
                    if b >= 4:
                        pe.wait_ge(s_sub, g * NB + b - 3)
                    for p in range(BP):
                        o = B[SCORE_BANKS[b % 4]][0:PAIR, p * PAIR:(p + 1) * PAIR]
                        ts = slice((b * BP + p) * 9, (b * BP + p + 1) * 9)
                        pe.matmul(o, blkb[:, 0:PAIR], blkb[:, PAIR:2 * PAIR], start=True, stop=False)
                        pe.matmul(o, qm[:, ts, :].rearrange("p t j -> p (t j)"),
                                  km[:, ts, :].rearrange("p t j -> p (t j)"), start=False, stop=False)
                        ins = pe.matmul(o, qr[:, ts, :].rearrange("p t j -> p (t j)"),
                                        kr[:, ts, :].rearrange("p t j -> p (t j)"), start=False, stop=True)
                    ins.then_inc(s_e, 1)

                def turn_probs(g, b):
                    pe.wait_ge(s_prob, g * NB + b + 1)
                    if not isinstance(g, int) or g or b >= 2:
                        pe.wait_ge(s_atsb, g * NB + b - 1)
                    for p in range(BP):
                        ins = pe.transpose(B[4 + b % 2][0:PAIR, p * PAIR:(p + 1) * PAIR], pr[:, b % 4, p, :],
                                           ident[0:PAIR, 0:PAIR])
                    ins.then_inc(s_at, 1)

                def weigh(g, b):
                    pe.wait_ge(s_atsb, g * NB + b + 1)
                    if not isinstance(g, int) or g or b:
                        pe.wait_ge(s_oa, g * NB + b)
                    for p in range(BP):
                        cs = slice(p * PAIR, (p + 1) * PAIR)
                        pe.matmul(B[6][:, cs], vp[:, b * BP + p, 0:DM], pt[:, b % 2, cs], start=True, stop=True)
                        ins = pe.matmul(B[7][0:DR, cs], vp[:, b * BP + p, DM:D], pt[:, b % 2, cs],
                                        start=True, stop=True)
                    ins.then_inc(s_o, 1)

                def group(g):
                    first = isinstance(g, int)
                    for i in range(NQK):
                        ring_free(g, i)
                        pe.matmul(bank(i)[:, 0:G], wqkm[:, i, :], x2Tm[:, ds(g * G, G)], start=True, stop=False)
                        pe.matmul(bank(i)[:, 0:G], wqkr[:, i, :], x2Tr[:, ds(g * G, G)],
                                  start=False, stop=True).then_inc(s_qk, 1)
                    if not first:
                        x3_turn(g - 1, NQK)
                    last = NQK if first else RING
                    pe.wait_ge(s_qka, evacuated("A", g, last))
                    pe.wait_ge(s_qkd, evacuated("D", g, last))
                    pe.wait_ge(s_vin, g * 16 + 16)
                    for b in range(AHEAD):
                        scores(g, b)
                    for b in range(NB + 1):
                        if b + AHEAD < NB:
                            scores(g, b + AHEAD)
                        if b < NB:
                            turn_probs(g, b)
                        if b >= 1:
                            weigh(g, b - 1)
                    pe.wait_ge(s_oa, g * NB + NB)
                    for t in range(NT):
                        for j in range(HEADS):
                            pe.matmul(tok_ps[:, t, :], om[:, t * T:(t + 1) * T, j], wpm[:, j, :],
                                      start=(j == 0), stop=False)
                            ins = pe.matmul(tok_ps[:, t, :], orr[:, t * T:(t + 1) * T, j], wpr[:, j, :],
                                            start=False, stop=(j == HEADS - 1))
                    ins.then_inc(s_proj, 1)

                pe.wait_ge(s_watt, 7 * 16)
                pe.wait_ge(s_blk, 1)
                group(0)
                with pe.Fori(1, NG) as g:
                    pe.wait_ge(s_hsum, g)
                    group(g)
                x3_turn(NG - 1, 0)

            def ring_item(eng, g, i, evac):
                eng.wait_ge(s_qk, items(g) + i + 1)
                m, r = (qm, qr) if i < NQK // 2 else (km, kr)
                p, w = (i % 12) // 3, i % 3
                wait(eng, s_e, g * NB)
                if w < 2:
                    return evac(m[:, :, 2 * p + w], bank(i)[:, 0:G], bqks[:, i:i + 1])
                evac(r[:, :, 2 * p], bank(i)[0:DR, 0:G], bqks[0:DR, i:i + 1])
                return evac(r[:, :, 2 * p + 1], bank(i)[DR:128, 0:G], bqks[DR:128, i:i + 1])

            @block.scalar
            def _(act):
                def evac(o, i, bias):
                    return act.activation(o, i, ACT.Identity, bias=bias)

                def root(g):
                    act.wait_ge(s_var, g + 1)
                    act.activation(std[:, :], ve[:, :], ACT.Sqrt).then_inc(s_std, 1)

                def x3_main(g, at):
                    act.wait_ge(s_qk, items(g + 1) + at + 1)
                    act.activation(x3Tm[:, ds(g * G, G)], bank(at)[:, 0:G], ACT.Copy).then_inc(s_qka, 1)

                def group(g):
                    for i in range(NQK):
                        if OWNER[i] == "A":
                            ring_item(act, g, i, evac).then_inc(s_qka, 1)
                        if i == 3 and not isinstance(g, int):
                            root(g - 1)
                    if not isinstance(g, int):
                        x3_main(g - 1, NQK)
                    for s in range(NB + 2):
                        if s < NB:
                            act.wait_ge(s_sub, g * NB + s + 1)
                            act.activation(pr[:, s % 4, :, :], pr[:, s % 4, :, :], ACT.Exp).then_inc(s_exp, 1)
                        if 1 <= s <= NB:
                            b = s - 1
                            act.wait_ge(s_at, g * NB + b + 1)
                            if not isinstance(g, int) or b >= 2:
                                act.wait_ge(s_o, g * NB + b - 1)
                            act.activation(pt[:, b % 2, :], B[4 + b % 2][0:PAIR, 0:BW], ACT.Copy).then_inc(s_atsb, 1)
                        if s >= 2:
                            b = s - 2
                            act.wait_ge(s_o, g * NB + b + 1)
                            if not isinstance(g, int):
                                act.wait_ge(s_proj, g)
                            act.activation(om[:, b * 36:(b + 1) * 36, :].rearrange("p t j -> p (t j)"),
                                           B[6][:, 0:BW], ACT.Copy, scale=float(D) ** -0.5)
                            act.activation(orr[:, b * 36:(b + 1) * 36, :].rearrange("p t j -> p (t j)"),
                                           B[7][0:DR, 0:BW], ACT.Copy, scale=float(D) ** -0.5).then_inc(s_oa, 1)

                group(0)
                with act.Fori(1, NG) as g:
                    group(g)
                root(NG - 1)
                x3_main(NG - 1, 0)

            @block.gpsimd
            def _(pool):
                with pool.Fori(0, NG) as g:
                    for b in range(NB):
                        pool.wait_ge(s_rec, g * NB + b + 1)
                        pool.tensor_tensor(pr[:, b % 4, :, :], pr[:, b % 4, :, :],
                                           ri[:, b % 4, :].unsqueeze(2).broadcast_to([PAIR, BP, PAIR]),
                                           ALU.mult).then_inc(s_prob, 1)

            @block.vector
            def _(dve):
                link = Chain(dve, s_dve)

                def evac(o, i, bias):
                    return dve.tensor_scalar(o, i, bias, None, ALU.add)

                def x3_rest(g, at):
                    dve.wait_ge(s_qk, items(g + 1) + at + 2)
                    dve.tensor_copy(x3Tr[:, ds(g * G, G)], bank(at + 1)[0:DR, 0:G]).then_inc(s_qkd, 1)

                def close(g):
                    link.loop(g, LN_LINKS + 1)
                    dve.wait_ge(s_proj, g + 1)
                    dve.tensor_tensor(hsum[:, :, :], tok_ps, bps[:, None, :].broadcast_to([T, NT, D]),
                                      ALU.add).then_inc(s_hsum, 1)
                    dve.wait_ge(s_hsum, g + 1)
                    hg = h_all[:, ds(g * NT, NT), :]
                    link(dve.tensor_tensor(hg, hg, hsum[:, :, :], ALU.add))

                    def xtok_free():
                        if not isinstance(g, int) or g > 0:
                            dve.wait_ge(s_qk, items(g) + RING)
                            dve.wait_ge(s_x3out, g * NT * 16)

                    layer_norm(dve, link, lambda t: h_all[:, ds(g * NT + t, 1), :].rearrange("p a d -> p (a d)"),
                               ln, g, s_var, s_std, xtok_free, s_xtok, spare)
                    link.end()

                def group(g):
                    for i in range(NQK):
                        if OWNER[i] == "D":
                            ring_item(dve, g, i, evac).then_inc(s_qkd, 1)
                    if not isinstance(g, int) or g > 0:
                        x3_rest(g - 1, NQK)
                    for s in range(NB + 1):
                        if s < NB:
                            sc = B[SCORE_BANKS[s % 4]][0:PAIR, 0:BW].rearrange("p (n k) -> p n k", n=BP)
                            dve.wait_ge(s_e, g * NB + s + 1)
                            dve.tensor_reduce(mx[:, s % 4, :], sc, AX.X, ALU.max).then_inc(s_max, 1)
                            dve.wait_ge(s_max, g * NB + s + 1)
                            if not isinstance(g, int) or g > 0 or s >= 4:
                                dve.wait_ge(s_at, g * NB + s - 3)
                            dve.tensor_tensor(pr[:, s % 4, :, :], sc,
                                              mx[:, s % 4, :].unsqueeze(2).broadcast_to([PAIR, BP, PAIR]),
                                              ALU.subtract).then_inc(s_sub, 1)
                        if s >= 1:
                            b = s - 1
                            dve.wait_ge(s_exp, g * NB + b + 1)
                            dve.tensor_reduce(sm[:, b % 4, :], pr[:, b % 4, :, :], AX.X, ALU.add).then_inc(s_sum, 1)
                            dve.wait_ge(s_sum, g * NB + b + 1)
                            if not isinstance(g, int) or g > 0 or b >= 4:
                                dve.wait_ge(s_prob, g * NB + b - 3)
                            dve.reciprocal(ri[:, b % 4, :], sm[:, b % 4, :]).then_inc(s_rec, 1)

                dve.tensor_copy(blkb[:, :], blk[:, :]).then_inc(s_blk, 1)
                group(0)
                close(0)
                group(1)
                with dve.Fori(2, NG) as g:
                    close(g - 1)
                    group(g)
                close(NG - 1)
                x3_rest(NG - 1, 0)

        with ExitStack() as st:
            def sb(name, shape, dt=F32):
                return st.enter_context(nc.sbuf_tensor(name, shape, dt))

            def sem(name):
                return st.enter_context(nc.semaphore(name))

            gm = sb("gm", [DM, E])
            gr = sb("gr", [DR, E])
            wsm = sb("wsm", [DM, 2 * F_SH])
            wsr = sb("wsr", [DR, 2 * F_SH])
            wsd = sb("wsd", [128, KS, D])
            sgate = sb("sgate", [128, 2, G])
            sup = sb("sup", [128, 2, G])
            sa = sb("sa", [128, KS, G])
            ysh = sb("ysh", [T, NT, D])
            sc = sb("sc", [E, N])
            tops = sb("tops", [E, CAP])
            topi = sb("topi", [E, CAP], U32)
            topf = sb("topf", [E, CAP])
            idx = sb("idx", [HC, 2, E], U32)
            scr = sb("scr", [HC, 2, E])
            idg = sb("idg", [HC, 2, 2], U32)
            ids = sb("ids", [HC, 2, 2], U32)
            wgm = [sb(f"wgm{u}", [DM, 2 * F_EXP]) for u in range(2)]
            wgr = [sb(f"wgr{u}", [DR, 2 * F_EXP]) for u in range(2)]
            wd = [sb(f"wd{u}", [128, KF, D]) for u in range(2)]
            xg = [sb(f"xg{u}", [HC, 2, D]) for u in range(2)]
            xgm = [sb(f"xgm{u}", [DM, CAP]) for u in range(2)]
            xgr = [sb(f"xgr{u}", [DR, CAP]) for u in range(2)]
            sl = sb("sl", [128, 2, 2, CAP])
            aT = [sb(f"aT{u}", [128, KF, CAP]) for u in range(2)]
            ys = [sb(f"ys{u}", [HC, 2, D]) for u in range(2)]

            s_ws = sem("s_ws")
            s_rps = sem("s_rps")
            s_sc = sem("s_sc")
            s_top = sem("s_top")
            s_topT = sem("s_topT")
            s_idx = sem("s_idx")
            s_sg = sem("s_sg")
            s_sga = sem("s_sga")
            s_sa = sem("s_sa")
            s_sd = sem("s_sd")
            s_sda = sem("s_sda")
            s_ysh = sem("s_ysh")
            s_init = sem("s_init")
            s_wgu = [sem(f"s_wgu{u}") for u in range(2)]
            s_wd = [sem(f"s_wd{u}") for u in range(2)]
            s_idg = sem("s_idg")
            s_ids = sem("s_ids")
            s_gath = [sem(f"s_gath{u}") for u in range(2)]
            s_xgt = sem("s_xgt")
            s_xga = sem("s_xga")
            s_xgd = sem("s_xgd")
            s_gu = sem("s_gu")
            s_silu = sem("s_silu")
            s_act = sem("s_act")
            s_y = sem("s_y")
            s_ys = sem("s_ys")
            s_scat = sem("s_scat")
            s_carry = sem("s_carry")
            block = st.enter_context(nc.Block())

            ITEMS = KF // 2

            @block.sync
            def _(sp):
                sp.dma_start(gm[:, :], gateT[0:DM, :]).then_inc(s_ws, 16)
                sp.dma_start(gr[:, :], gateT[DM:D, :]).then_inc(s_ws, 16)
                sp.dma_start(wsm[:, :], Wsgu[0:DM, :]).then_inc(s_ws, 16)
                sp.dma_start(wsr[:, :], Wsgu[DM:D, :]).then_inc(s_ws, 16)
                sp.dma_start(wsd[:, :, :], Wsd).then_inc(s_ws, 16)

                def load_gu(e, u):
                    sp.dma_start(wgm[u][:, :], Wgu[ds(e, 1), 0:DM, :].rearrange("a p f -> (a p) f")).then_inc(s_wgu[u], 16)
                    sp.dma_start(wgr[u][:, :], Wgu[ds(e, 1), DM:D, :].rearrange("a p f -> (a p) f")).then_inc(s_wgu[u], 16)

                def load_d(e, u):
                    sp.dma_start(wd[u][:, :, :], Wd[ds(e, 1)].rearrange("a p k d -> (a p) k d")).then_inc(s_wd[u], 16)

                for e in range(2):
                    load_gu(e, e)
                    load_d(e, e)
                with sp.Fori(0, NG) as g:
                    sp.wait_ge(s_ysh, g + 1)
                    for t in range(NT):
                        sp.dma_start(out_rows[ds(g * G + t * T, T), :], ysh[:, t, :]).then_inc(s_init, 16)
                with sp.Fori(1, E // 2) as i:
                    for u in range(2):
                        e = 2 * i + u
                        sp.wait_ge(s_gu, (e - 2) * ITEMS + ITEMS)
                        load_gu(e, u)
                        sp.wait_ge(s_y, e - 1)
                        load_d(e, u)

            @block.tensor
            def _(pe):
                pe.wait_ge(s_ws, 5 * 16)
                for c in range(3):
                    cs = slice(c * 384, (c + 1) * 384)
                    pe.matmul(B[5 + c][0:E, 0:384], gm[:, :], x3Tm[:, cs], start=True, stop=False)
                    ins = pe.matmul(B[5 + c][0:E, 0:384], gr[:, :], x3Tr[:, cs], start=False, stop=True)
                ins.then_inc(s_rps, 1)
                def shared(g):
                    xm, xr = x3Tm[:, ds(g * G, G)], x3Tr[:, ds(g * G, G)]
                    for m in range(KS):
                        wait(pe, s_sga, g * KS + m)
                        for w in range(2):
                            o = B[w][:, 0:G]
                            fs = slice(w * F_SH + m * 128, w * F_SH + (m + 1) * 128)
                            pe.matmul(o, wsm[:, fs], xm, start=True, stop=False)
                            ins = pe.matmul(o, wsr[:, fs], xr, start=False, stop=True)
                        ins.then_inc(s_sg, 1)
                    pe.wait_ge(s_sa, g * KS + KS)
                    wait(pe, s_sda, g * NT)
                    for t in range(NT):
                        for k in range(KS):
                            ins = pe.matmul(B[2 + t][0:T, 0:D], sa[:, k, t * T:(t + 1) * T], wsd[:, k, :],
                                            start=(k == 0), stop=(k == KS - 1))
                    ins.then_inc(s_sd, 1)

                shared(0)
                with pe.Fori(1, NG) as g:
                    shared(g)
                pe.wait_ge(s_top, 3 * ROUNDS + 1)
                pe.wait_ge(s_sc, 3)
                for n in range(2):
                    for h in range(2):
                        src = (topf, tops)[n]
                        ins = pe.transpose(B[5][0:HC, (2 * n + h) * E:(2 * n + h + 1) * E],
                                           src[:, h * HC:(h + 1) * HC], ident[0:E, 0:E])
                ins.then_inc(s_topT, 1)
                pe.wait_ge(s_idx, 2)

                def turn_tokens(i, u):
                    e = 2 * i + u
                    pe.wait_ge(s_gath[u], 32 * i + 32)
                    wait(pe, s_xga, e)
                    wait(pe, s_xgd, e)
                    for h in range(2):
                        pe.transpose(B[5][:, h * HC:(h + 1) * HC], xg[u][:, h, 0:DM], ident[0:HC, 0:HC])
                        ins = pe.transpose(B[4][0:DR, h * HC:(h + 1) * HC], xg[u][:, h, DM:D],
                                           ident[0:HC, 0:HC])
                    ins.then_inc(s_xgt, 1)

                def gate_up(e, u, n):
                    r = (ITEMS * u + n) % 2
                    if not isinstance(e, int) or e * ITEMS + n >= 2:
                        pe.wait_ge(s_act, e * ITEMS + n - 1)
                    for w in range(2):
                        for m in range(2):
                            o = B[2 * w + r][:, m * CAP:(m + 1) * CAP]
                            f = w * F_EXP + (2 * n + m) * 128
                            pe.matmul(o, wgm[u][:, f:f + 128], xgm[u][:, :], start=True, stop=False)
                            ins = pe.matmul(o, wgr[u][:, f:f + 128], xgr[u][:, :], start=False, stop=True)
                    ins.then_inc(s_gu, 1)

                def down(i, u):
                    e = 2 * i + u
                    pe.wait_ge(s_wd[u], 16 * i + 16)
                    pe.wait_ge(s_act, e * ITEMS + ITEMS)
                    if not isinstance(e, int) or e >= 2:
                        pe.wait_ge(s_ys, 2 * e - 2)
                    for h in range(2):
                        for k in range(KF):
                            ins = pe.matmul(B[6 + u][0:HC, h * 256:h * 256 + D], aT[u][:, k, h * HC:(h + 1) * HC],
                                            wd[u][:, k, :], start=(k == 0), stop=(k == KF - 1))
                    ins.then_inc(s_y, 1)

                def turn(i, u):
                    e = 2 * i + u
                    pe.wait_ge(s_xga, e + 1)
                    pe.wait_ge(s_xgd, e + 1)
                    pe.wait_ge(s_wgu[u], 32 * i + 32)
                    gate_up(e, u, 0)
                    if not isinstance(e, int) or e > 0:
                        down(*((i, 0) if u else (i - 1, 1)))
                    gate_up(e, u, 1)
                    if not isinstance(e, int) or e < E - 1:
                        turn_tokens(*((i + 1, 0) if u else (i, 1)))
                    gate_up(e, u, 2)

                turn_tokens(0, 0)
                turn(0, 0)
                turn(0, 1)
                with pe.Fori(1, E // 2 - 1) as i:
                    turn(i, 0)
                    turn(i, 1)
                turn(E // 2 - 1, 0)
                turn(E // 2 - 1, 1)
                down(E // 2 - 1, 1)

            @block.scalar
            def _(act):
                act.wait_ge(s_rps, 1)
                for c in range(3):
                    act.activation(sc[:, c * 384:(c + 1) * 384], B[5 + c][0:E, 0:384], ACT.Sigmoid).then_inc(s_sc, 1)
                def shared(g):
                    for m in range(KS):
                        i = g * KS + m
                        act.wait_ge(s_sg, i + 1)
                        wait(act, s_sa, i)
                        act.activation(sgate[:, 0, :], B[0][:, 0:G], ACT.Silu)
                        act.activation(sup[:, 0, :], B[1][:, 0:G], ACT.Copy).then_inc(s_sga, 1)
                    act.wait_ge(s_sd, g + 1)
                    wait(act, s_init, g * NT * 16)
                    wait(act, s_ysh, g)
                    for t in range(NT):
                        act.activation(ysh[:, t, :], B[2 + t][0:T, 0:D], ACT.Copy).then_inc(s_sda, 1)

                shared(0)
                with act.Fori(1, NG) as g:
                    shared(g)

                def tokens_main(e, u):
                    act.wait_ge(s_xgt, e + 1)
                    act.activation(xgm[u][:, :], B[5][:, 0:CAP], ACT.Copy).then_inc(s_xga, 1)

                def silu(e, u, n):
                    r = (ITEMS * u + n) % 2
                    act.wait_ge(s_gu, e * ITEMS + n + 1)
                    act.activation(sl[:, r, :, :], B[r][:, 0:2 * CAP].rearrange("p (m c) -> p m c", m=2),
                                   ACT.Silu).then_inc(s_silu, 1)

                def turn(i, u):
                    e = 2 * i + u
                    silu(e, u, 0)
                    silu(e, u, 1)
                    if not isinstance(e, int) or e < E - 1:
                        tokens_main(e + 1, 1 - u)
                    silu(e, u, 2)

                tokens_main(0, 0)
                with act.Fori(0, E // 2 - 1) as i:
                    turn(i, 0)
                    turn(i, 1)
                turn(E // 2 - 1, 0)
                turn(E // 2 - 1, 1)

            @block.gpsimd
            def _(pool):
                def shared(g):
                    for m in range(KS):
                        pool.wait_ge(s_sga, g * KS + m + 1)
                        wait(pool, s_sd, g)
                        pool.tensor_tensor(sa[:, m, :], sgate[:, 0, :], sup[:, 0, :], ALU.mult).then_inc(s_sa, 1)
                    pool.wait_ge(s_sda, g * NT + NT)
                    pool.tensor_tensor(ysh[:, :, :], ysh[:, :, :], h_all[:, ds(g * NT, NT), :],
                                       ALU.add).then_inc(s_ysh, 1)

                shared(0)
                with pool.Fori(1, NG) as g:
                    shared(g)
                pool.wait_ge(s_idx, 2)

                def carry_wait(n):
                    wait(pool, s_carry, n)
                    pool.tensor_tensor(pspare[:, 0:1], pspare[:, 1:2], pspare[:, 1:2], ALU.mult).then_inc(s_carry, 1)

                def gather(e, u, n):
                    if not isinstance(e, int) or e >= 2:
                        pool.wait_ge(s_xgt, e - 1)
                    pool.tensor_copy(idg[:, u, :], idx[:, :, ds(e, 1)].rearrange("p h a -> p (h a)")).then_inc(s_idg, 1)
                    pool.wait_ge(s_idg, e + 1)
                    carry_wait(n)
                    for h in range(2):
                        pool.indirect_dma_start(xg[u][:, h, :], None, x3_dram,
                                                bass.IndirectOffsetOnAxis(ap=idg[:, u, h:h + 1], axis=0)
                                                ).then_inc(s_gath[u], 16)

                def scatter(e, u, n):
                    pool.wait_ge(s_ys, 2 * e + 2)
                    wait(pool, s_scat, e * 32)
                    pool.tensor_copy(ids[:, u, :], idx[:, :, ds(e, 1)].rearrange("p h a -> p (h a)")).then_inc(s_ids, 1)
                    pool.wait_ge(s_ids, e + 1)
                    carry_wait(n)
                    for h in range(2):
                        pool.indirect_dma_start(out_rows, bass.IndirectOffsetOnAxis(ap=ids[:, u, h:h + 1], axis=0),
                                                ys[u][:, h, :], None, compute_op=ALU.add).then_inc(s_scat, 16)

                gather(0, 0, 0)
                gather(1, 1, 1)
                gather(2, 0, 2)
                pool.wait_ge(s_init, NG * NT * 16)
                scatter(0, 0, 3)
                gather(3, 1, 4)
                with pool.Fori(1, E // 2 - 1) as i:
                    scatter(2 * i - 1, 1, 4 * i + 1)
                    gather(2 * i + 2, 0, 4 * i + 2)
                    scatter(2 * i, 0, 4 * i + 3)
                    gather(2 * i + 3, 1, 4 * i + 4)
                for e in range(E - 3, E):
                    scatter(e, e % 2, E + e)
                pool.wait_ge(s_scat, E * 32)

            @block.vector
            def _(dve):
                dve.wait_ge(s_sc, 3)
                for r in range(ROUNDS):
                    rs8 = slice(8 * r, 8 * r + 8)
                    dve.max(tops[:, rs8], sc[:, :]).then_inc(s_top, 1)
                    dve.wait_ge(s_top, 3 * r + 1)
                    dve.max_index(topi[:, rs8], tops[:, rs8], sc[:, :]).then_inc(s_top, 1)
                    dve.wait_ge(s_top, 3 * r + 2)
                    dve.match_replace(sc[:, :], tops[:, rs8], sc[:, :], -1.0).then_inc(s_top, 1)
                    dve.wait_ge(s_top, 3 * r + 3)
                dve.tensor_copy(topf[:, :], topi[:, :]).then_inc(s_top, 1)
                dve.wait_ge(s_topT, 1)
                dve.tensor_copy(idx[:, :, :], B[5][0:HC, 0:2 * E].rearrange("p (h e) -> p h e", h=2)).then_inc(s_idx, 1)
                dve.tensor_copy(scr[:, :, :], B[5][0:HC, 2 * E:4 * E].rearrange("p (h e) -> p h e", h=2)).then_inc(s_idx, 1)
                dve.wait_ge(s_idx, 2)

                def tokens_rest(e, u):
                    dve.wait_ge(s_xgt, e + 1)
                    dve.tensor_copy(xgr[u][:, :], B[4][0:DR, 0:CAP]).then_inc(s_xgd, 1)

                def product(e, u, n):
                    r = (ITEMS * u + n) % 2
                    dve.wait_ge(s_silu, e * ITEMS + n + 1)
                    dve.tensor_tensor(aT[u][:, 2 * n:2 * n + 2, :],
                                      B[2 + r][:, 0:2 * CAP].rearrange("p (m c) -> p m c", m=2),
                                      sl[:, r, :, :], ALU.mult).then_inc(s_act, 1)

                def weighted(e, u):
                    dve.wait_ge(s_y, e + 1)
                    if not isinstance(e, int) or e >= 2:
                        dve.wait_ge(s_scat, 32 * (e - 1))
                    for h in range(2):
                        dve.tensor_scalar(ys[u][:, h, :], B[6 + u][0:HC, h * 256:h * 256 + D],
                                          scr[:, h, ds(e, 1)], None, ALU.mult).then_inc(s_ys, 1)

                def turn(i, u):
                    e = 2 * i + u
                    product(e, u, 0)
                    if not isinstance(e, int) or e > 0:
                        weighted(e - 1, 1 - u)
                    product(e, u, 1)
                    if not isinstance(e, int) or e < E - 1:
                        tokens_rest(e + 1, 1 - u)
                    product(e, u, 2)

                tokens_rest(0, 0)
                turn(0, 0)
                turn(0, 1)
                with dve.Fori(1, E // 2 - 1) as i:
                    turn(i, 0)
                    turn(i, 1)
                turn(E // 2 - 1, 0)
                turn(E // 2 - 1, 1)
                weighted(E - 1, 1)


def kernel(**inputs):
    import numpy as _np
    import concourse.bacc as _bacc
    from concourse import mybir as _mybir
    from concourse.bass_utils import run_bass_kernel_spmd as _run

    a = {k: _np.asarray(v) for k, v in inputs.items()}
    x = a["x"].reshape(IMAGES, 3, 6, PATCH, 6, PATCH).transpose(0, 2, 4, 1, 3, 5).reshape(NG, G, KI, 128)
    Wq, Wk, Wv = _np.split(a["L0_attn_W_qkv"], 3, axis=1)
    bq, bk, bv = _np.split(a["L0_attn_b_qkv"], 3)

    def tiles(w):
        w = w.reshape(-1, 4, 2, D)
        rest = w[:, :, :, DM:].reshape(-1, 4, 1, 128)
        return _np.concatenate([w[:, :, :, :DM], rest], axis=2).reshape(-1, 12, 128)

    rows = _np.arange(PAIR) < PAIR // 2
    blocks = _np.zeros((2, 2 * PAIR), _np.float32)
    blocks[0, :PAIR], blocks[1, :PAIR] = rows, ~rows
    blocks[0, PAIR:], blocks[1, PAIR:] = _np.where(~rows, -1e30, 0), _np.where(rows, -1e30, 0)
    arrays = {
        "xT": x.transpose(0, 3, 2, 1),
        "W1": a["L0_tok_W1"].reshape(KI, 128, KH, 128).transpose(2, 1, 0, 3),
        "b1": a["L0_tok_b1"].reshape(KH, 128).T,
        "W2": a["L0_tok_W2"].reshape(KH, 128, D).transpose(1, 0, 2),
        "b2": a["L0_tok_b2"],
        "Wqk": _np.concatenate([tiles(Wq), tiles(Wk)], axis=1),
        "bqk": _np.concatenate([tiles(bq), tiles(bk)], axis=1)[0].T,
        "Wv": Wv, "bv": bv,
        "Wp": a["L0_attn_W_proj"].reshape(HEADS, D, D).transpose(1, 0, 2),
        "bp": a["L0_attn_b_proj"],
        "blocks": blocks,
        "gateT": a["L0_ffn_gate_weight"].T,
        "Wgu": _np.concatenate([a["L0_ffn_Wg"].transpose(0, 2, 1), a["L0_ffn_Wu"].transpose(0, 2, 1)], axis=2),
        "Wd": a["L0_ffn_Wd"].transpose(0, 2, 1).reshape(E, KF, 128, D).transpose(0, 2, 1, 3),
        "Wsgu": _np.concatenate([a["L0_ffn_Ws_g"].T, a["L0_ffn_Ws_u"].T], axis=1),
        "Wsd": a["L0_ffn_Ws_d"].T.reshape(KS, 128, D).transpose(1, 0, 2),
    }
    nc = _bacc.Bacc("TRN2", target_bir_lowering=False, num_devices=1)
    feed, args = {}, []
    for name, v in arrays.items():
        v = _np.ascontiguousarray(v)
        feed[f"in_{name}"] = v
        args.append(nc.dram_tensor(f"in_{name}", v.shape, _mybir.dt.from_np(v.dtype), kind="ExternalInput").ap())
    args.append(nc.dram_tensor("out_0", (IMAGES, SEQ, D), _mybir.dt.float32, kind="ExternalOutput").ap())
    vit_moe_kernel(nc, *args)
    r = _run(nc, [feed], core_ids=[0])
    return r.results[0]["out_0"]
```

```python
from contextlib import ExitStack

import concourse.bass as bass
import concourse.mybir as mybir

F32 = mybir.dt.float32
F32R = mybir.dt.float32r
BF16 = mybir.dt.bfloat16
U32 = mybir.dt.uint32
ACT = mybir.ActivationFunctionType
ALU = mybir.AluOpType
AX = mybir.AxisListType

IMAGES, SEQ, D = 32, 36, 192
N = IMAGES * SEQ
PATCH = 16
IN_DIM = 3 * PATCH * PATCH
HID = 768
HEADS = 8
QKV = HEADS * D
E, F_EXP, TOP_K, F_SH = 16, 768, 2, 384
CAP = N * TOP_K // E
EPS = 1e-5

G = 288
NG = N // G
T = 96
NT = G // T
KI = IN_DIM // 128
KH = HID // 128
DM, DR = 128, D - 128
PAIR = 72
BP = 4
NB = G // 9 // BP
BW = BP * PAIR
NQK = 24
HC = CAP // 2
KF = F_EXP // 128
KS = F_SH // 128
ROUNDS = CAP // 8
WC = 768
NQC = 2 * QKV // WC
XC = KI // 2
NA = N // 2
ds = bass.ds


def wait(eng, sem, value):
    if not isinstance(value, int) or value > 0:
        eng.wait_ge(sem, value)


class Chain:

    def __init__(self, eng, sem, start=0):
        self.eng, self.sem, self.n, self.off = eng, sem, start, 0

    def __call__(self, ins):
        self.n += 1
        ins.then_inc(self.sem, 1)
        self.eng.wait_ge(self.sem, self.off + self.n)

    def loop(self, turn, per):
        self.n, self.per, self.off = 0, per, turn * per

    def end(self):
        assert self.n == self.per, (self.n, self.per)


def in_parts(pe, out, x, w, start, stop, w_stationary=False):
    (xh, xl, xs), (wh, wl, whh, wrl) = x, w
    passes = [(xh, wh), (xl, wh), (xh, wl), (xs, whh), (xs[0:DR], wrl)]
    for n, (a, b) in enumerate(passes):
        a, b = (b, a) if w_stationary else (a, b)
        ins = pe.matmul(out, a, b, start=(start and n == 0), stop=(stop and n == len(passes) - 1))
    return ins


class Pick:

    def __init__(self, dve, scores, tops, topi, s_top):
        self.dve, self.scores, self.tops, self.topi, self.s_top, self.n = dve, scores, tops, topi, s_top, 0

    def steps(self, count):
        dve = self.dve
        for n in range(self.n, self.n + count):
            rs8 = slice(8 * (n // 3), 8 * (n // 3) + 8)
            if n % 3 == 0:
                ins = dve.max(self.tops[:, rs8], self.scores)
            elif n % 3 == 1:
                ins = dve.max_index(self.topi[:, rs8], self.tops[:, rs8], self.scores)
            else:
                ins = dve.match_replace(self.scores, self.tops[:, rs8], self.scores, -1.0)
            ins.then_inc(self.s_top, 1)
            dve.wait_ge(self.s_top, n + 1)
        self.n += count


def layer_norm(dve, link, src, ln, turn, s_var, s_std, s_xtok, spare):
    dve.memset(spare, 0.0)
    for t in range(NT):
        dve.bn_stats(ln["stats"][:, t, :], src(t)).then_inc(ln["s_stat"], 1)
    dve.wait_ge(ln["s_stat"], turn * NT + NT)
    dve.memset(spare, 0.0)
    for t in range(NT - 1):
        dve.bn_aggr(ln["mv"][:, t, :], ln["stats"][:, t, :])
    link(dve.bn_aggr(ln["mv"][:, NT - 1, :], ln["stats"][:, NT - 1, :]))
    ve, std, rs, rt = ln["ve"], ln["std"], ln["rs"], ln["rt"]
    dve.tensor_scalar(ve[:, :], ln["mv"][:, :, 1], EPS, None, ALU.add).then_inc(s_var, 1)
    dve.wait_ge(s_std, turn + 1)
    link(dve.reciprocal(rs[:, :], std[:, :]))
    link(dve.tensor_tensor(rt[:, :], rs[:, :], rs[:, :], ALU.mult))
    link(dve.tensor_tensor(rt[:, :], rt[:, :], ve[:, :], ALU.mult))
    link(dve.tensor_scalar(rt[:, :], rt[:, :], -0.5, 1.5, ALU.mult, ALU.add))
    link(dve.tensor_tensor(rs[:, :], rs[:, :], rt[:, :], ALU.mult))
    for t in range(NT):
        ins = dve.tensor_scalar(ln["xtok"][:, t, :], src(t), ln["mv"][:, t, 0:1], rs[:, t:t + 1],
                                ALU.subtract, ALU.mult)
        ins.then_inc(s_xtok, 1)


LN_LINKS = 6

OWNER = "AAAAAAAADADADADADADADADA" + "AD"
RING = len(OWNER)
RING_BANKS = [2, 3, 4, 5]
SCORE_BANKS = [2, 3, 0]
NSB = len(SCORE_BANKS)
PICKS_2 = [0, 0, 3, 3, 3, 3, 3, 6]
PICKS_3 = [3, 3, 2, 2, 2, 2, 6, 6]
AHEAD = 2


def owned(who, i):
    return OWNER[:i].count(who)


def vit_moe_kernel(nc, xT, W1, b1, W2, b2, Wqp, bqk, Wv, bv, bp, blocks, gateT, Wgu, Wd, Wsgu, Wsd, out):
    with ExitStack() as ctx:
        def sb(name, shape, dt=F32):
            return ctx.enter_context(nc.sbuf_tensor(name, shape, dt))

        def sem(name):
            return ctx.enter_context(nc.semaphore(name))

        out_rows = out.rearrange("a b c -> (a b) c")
        v_dram = nc.dram_tensor("v_scratch", [N, QKV], F32, kind="Internal").ap()
        x3_dram = nc.dram_tensor("x3_scratch", [N, D], F32, kind="Internal").ap()

        ident = sb("ident", [128, 128])
        h_all = sb("h_all", [T, NG * NT, D])
        x3Tm = sb("x3Tm", [DM, N])
        x3Tr128 = sb("x3Tr", [128, N])
        x3Tr = x3Tr128[0:DR]
        spare = sb("spare", [1, 1])[:, :]
        pspare = sb("pspare", [1, 2])
        ln = {"stats": sb("stats", [T, NT, 6]), "mv": sb("mv", [T, NT, 2]), "ve": sb("ve", [T, NT]),
              "std": sb("std", [T, NT]), "rs": sb("rs", [T, NT]), "rt": sb("rt", [T, NT]),
              "xtok": sb("xtok", [T, NT, D])}
        xtok, ve, std = ln["xtok"], ln["ve"], ln["std"]
        hsum = xtok
        raw = [x3Tm, x3Tr128]

        B = [ctx.enter_context(nc.psum_tensor(f"bank{i}", [128, 512], F32)) for i in range(6)]
        ps67 = ctx.enter_context(nc.psum_tensor("bank67", [128, 1024], F32))
        B += [ps67[:, 0:512], ps67[:, 512:1024]]
        tok_ps = ps67[0:T, 0:NT * 256].rearrange("p (t c) -> p t c", t=NT)[:, :, 0:D]

        bps = sb("bps", [T, D])
        gm = sb("gm", [DM, 128])
        gr = sb("gr", [DR, 128])
        sel = x3Tr128[DR:DR + E]
        scA = sel[:, 0:NA]
        topsA, topiA = sel[:, N - 2 * CAP:N - CAP], sel[:, N - CAP:N].bitcast(U32)

        s_watt = sem("s_watt")
        s_vout = [sem(f"s_vout{t}") for t in range(NT)]
        s_x3out = sem("s_x3out")
        s_rps = sem("s_rps")
        s_sc = sem("s_sc")
        s_topA = sem("s_topA")
        s_rawm = sem("s_rawm")
        s_rawr = sem("s_rawr")
        s_him = sem("s_him")
        s_hir = sem("s_hir")
        s_spm = sem("s_spm")
        s_spr = sem("s_spr")

        attn = ctx.enter_context(ExitStack())

        def sb(name, shape, dt=F32):
            return attn.enter_context(nc.sbuf_tensor(name, shape, dt))

        x2h = sb("x2h", [DM, N], F32R)
        x2l = sb("x2l", [DM, N], F32R)
        x2s = sb("x2s", [128, N], F32R)
        wh = sb("wh", [DM, 2 * QKV], F32R)
        wl = sb("wl", [DM, 2 * QKV], F32R)
        whh = sb("whh", [128, 2 * QKV], F32R)
        wrl = sb("wrl", [DR, 2 * QKV], F32R)
        qk_parts = (wh, wl, whh, wrl)
        bqks = sb("bqks", [128, NQK])
        blk = sb("blk", [2, 2 * PAIR])

        def logits(pe, out, ts):
            pe.matmul(out, gm[:, :], x3Tm[:, ts], start=True, stop=False)
            return pe.matmul(out, gr[:, :], x3Tr[:, ts], start=False, stop=True)

        def load_raw(sp, c):
            cs = ds(c * WC, WC)
            wait(sp, s_spm, c)
            sp.dma_start(raw[0][:, 0:WC], Wqp[0:DM, cs]).then_inc(s_rawm, 16)
            wait(sp, s_spr, c)
            sp.dma_start(raw[1][0:DR, 0:WC], Wqp[DM:D, cs]).then_inc(s_rawr, 16)
            sp.dma_start(raw[1][DR:128, 0:WC], Wqp[DM:D, cs]).then_inc(s_rawr, 16)

        def high_parts(act, c, parts, at):
            cs = ds(at * WC, WC)
            act.wait_ge(s_rawm, 16 * c + 16)
            act.activation(parts[0][:, cs], raw[0][:, 0:WC], ACT.Copy).then_inc(s_him, 1)
            act.wait_ge(s_rawr, 32 * c + 32)
            act.activation(parts[2][:, cs], raw[1][:, 0:WC], ACT.Copy).then_inc(s_hir, 1)

        def low_main(pool, c, parts, at):
            cs = ds(at * WC, WC)
            pool.wait_ge(s_him, c + 1)
            pool.tensor_tensor(parts[1][:, cs], raw[0][:, 0:WC], parts[0][:, cs].bitcast(F32),
                               ALU.subtract).then_inc(s_spm, 1)

        def low_rest(pool, c, parts, at):
            cs = ds(at * WC, WC)
            pool.wait_ge(s_hir, c + 1)
            pool.tensor_tensor(parts[3][:, cs], raw[1][0:DR, 0:WC], parts[2][0:DR, cs].bitcast(F32),
                               ALU.subtract).then_inc(s_spr, 1)

        with ExitStack() as st:
            def sb(name, shape, dt=F32):
                return st.enter_context(nc.sbuf_tensor(name, shape, dt))

            def sem(name):
                return st.enter_context(nc.semaphore(name))

            xraw = sb("xraw", [128, KI, G])
            xh = sb("xh", [128, KI, G], F32R)
            xl = sb("xl", [128, KI, G], F32R)
            w1h = sb("w1h", [128, KH, KI, 128], F32R)
            w1l = sb("w1l", [128, KH, KI, 128], F32R)
            w2 = sb("w2", [128, KH, D])
            b1s = sb("b1s", [128, KH])
            b2s = sb("b2s", [T, D])
            wvh = sb("wvh", [DM, QKV], F32R)
            wvl = sb("wvl", [DM, QKV], F32R)
            wvhh = sb("wvhh", [128, QKV], F32R)
            wvrl = sb("wvrl", [DR, QKV], F32R)
            bvs = sb("bvs", [T, QKV])
            hT = sb("hT", [128, KH, G])
            x2gh = sb("x2gh", [DM, G], F32R)
            x2gl = sb("x2gl", [DM, G], F32R)
            x2gs = sb("x2gs", [128, G], F32R)
            vtok = sb("vtok", [128, NT, QKV])
            w1 = vtok[:, :, :].rearrange("p t c -> p (t c)").rearrange("p (m k f) -> p m k f", m=KH, k=KI)

            s_id = sem("s_id")
            s_x0 = sem("s_x0")
            s_x = sem("s_x")
            s_xh = sem("s_xh")
            s_xl0 = sem("s_xl0")
            s_xl = sem("s_xl")
            s_w1h = sem("s_w1h")
            s_w1l = sem("s_w1l")
            s_w1 = [sem(f"s_w1_{m}") for m in range(KH)]
            s_small = sem("s_small")
            s_smalld = sem("s_smalld")
            s_w2 = sem("s_w2")
            s_tok1 = sem("s_tok1")
            s_hT = sem("s_hT")
            s_tok2 = sem("s_tok2")
            s_hsum = sem("s_hsum")
            s_var = sem("s_var")
            s_std = sem("s_std")
            s_xtok = sem("s_xtok")
            s_x2ps = sem("s_x2ps")
            s_x2a = sem("s_x2a")
            s_x2d = sem("s_x2d")
            s_x2T = sem("s_x2T")
            s_v = sem("s_v")
            s_vsb = sem("s_vsb")
            s_rawv = sem("s_rawv")
            s_vhi = sem("s_vhi")
            s_vlo = sem("s_vlo")
            s_dve = sem("s_dve")
            ln["s_stat"] = sem("s_stat")
            block = st.enter_context(nc.Block())

            @block.sync
            def _(sp):
                def load_x(g):
                    sp.dma_start(xraw[:, :, :], xT[g]).then_inc(s_x, 16)

                sp.dma_start(xraw[:, 0:XC, :], xT[0][:, 0:XC, :]).then_inc(s_x0, 16)
                for m in range(KH):
                    sp.dma_start(w1[:, m, :, :], W1[m]).then_inc(s_w1[m], 16)
                    if m == 0:
                        sp.dma_start(xraw[:, XC:KI, :], xT[0][:, XC:KI, :]).then_inc(s_x, 16)
                    if m == 1:
                        sp.dma_start(b1s[:, :], b1).then_inc(s_small, 16)
                sp.dma_start(w2[:, :, :], W2).then_inc(s_w2, 16)
                sp.dma_start(b2s[:, :], b2.partition_broadcast(T)).then_inc(s_smalld, 16)
                sp.dma_start(bvs[:, :], bv.partition_broadcast(T)).then_inc(s_smalld, 16)
                sp.wait_ge(s_xl0, 2)
                load_x(1)
                load_raw(sp, 0)
                sp.wait_ge(s_w1l, KH)
                sp.dma_start(vtok[:, 0, :], Wv[0:DM, :]).then_inc(s_rawv, 16)
                sp.dma_start(vtok[0:DR, 1, :], Wv[DM:D, :]).then_inc(s_rawv, 16)
                sp.dma_start(vtok[DR:128, 1, :], Wv[DM:D, :]).then_inc(s_rawv, 16)
                sp.wait_ge(s_xl, 2)
                load_x(2)
                load_raw(sp, 1)
                sp.dma_start(bqks[:, :], bqk).then_inc(s_watt, 16)
                sp.dma_start(bps[:, :], bp.partition_broadcast(T)).then_inc(s_watt, 16)
                sp.dma_start(blk[:, :], blocks).then_inc(s_watt, 16)
                sp.wait_ge(s_id, 1)
                sp.dma_start(gm[:, 0:E], gateT[0:DM, :]).then_inc(s_watt, 16)
                sp.dma_start(gr[:, 0:E], gateT[DM:D, :]).then_inc(s_watt, 16)

                def stores(g):
                    for t in range(NT):
                        sp.wait_ge(s_vsb, g * 9 + 3 * t + 3)
                        sp.dma_start(v_dram[ds(g * G + t * T, T), :], vtok[0:T, t, :]).then_inc(s_vout[t], 16)

                stores(0)
                sp.wait_ge(s_xl, 4)
                load_x(3)
                load_raw(sp, 2)
                stores(1)
                load_raw(sp, 3)
                stores(2)
                stores(3)
                for t in range(NT):
                    sp.wait_ge(s_vout[t], 16 * NG)
                sp.wait_ge(s_watt, 5 * 16)

            @block.gpsimd
            def _(pool):
                pool.memset(pspare[:, :], 0.0)
                pool.memset(gm[:, :], 0.0)
                pool.memset(gr[:, :], 0.0)
                pool.memset(ident[:, :], 0.0).then_inc(s_id, 1)
                pool.wait_ge(s_id, 1)
                pool.affine_select(out=ident[:, :], in_=ident[:, :], compare_op=ALU.not_equal, fill=1.0, base=0,
                                   pattern=[[-1, 128]], channel_multiplier=1).then_inc(s_id, 1)

                def copies(g):
                    pool.wait_ge(s_x2d, g * 2 + 2)
                    for o, i in ((x2h, x2gh), (x2l, x2gl), (x2s, x2gs)):
                        pool.tensor_copy(o[:, ds(g * G, G)], i[:, :]).then_inc(s_x2T, 1)

                def x_low(g):
                    for c in range(2):
                        ks = slice(c * XC, (c + 1) * XC)
                        pool.wait_ge(s_xh, 2 * g + c + 1)
                        pool.tensor_tensor(xl[:, ks, :], xraw[:, ks, :], xh[:, ks, :].bitcast(F32),
                                           ALU.subtract).then_inc(s_xl, 1)

                x_low(1)
                with pool.Fori(0, NG - 2) as g:
                    low_main(pool, g, qk_parts, g)
                    low_rest(pool, g, qk_parts, g)
                    copies(g)
                    x_low(g + 2)
                for g in (NG - 2, NG - 1):
                    low_main(pool, g, qk_parts, g)
                    low_rest(pool, g, qk_parts, g)
                    copies(g)

            @block.tensor
            def _(pe):
                def tok1(g):
                    for m in range(KH):
                        if isinstance(g, int) and g == 0:
                            pe.wait_ge(s_w1l, m + 1)
                        elif m == 0:
                            pe.wait_ge(s_xl, 2 * g)
                        wait(pe, s_hT, g * KH + m - 1)
                        parts = [(w, x, k) for k in range(KI) for w, x in ((w1h, xh), (w1l, xh), (w1h, xl))]
                        for n, (w, x, k) in enumerate(parts):
                            if isinstance(g, int) and g == 0 and m == 0 and n % (3 * XC) == 0:
                                pe.wait_ge(s_xl0, k // XC + 1)
                            ins = pe.matmul(B[m % 2][:, 0:G], w[:, m, k, :], x[:, k, :],
                                            start=(n == 0), stop=(n == len(parts) - 1))
                        ins.then_inc(s_tok1, 1)

                def tok2(g):
                    pe.wait_ge(s_hT, g * KH + KH)
                    wait(pe, s_hsum, g)
                    for t in range(NT):
                        for k in range(KH):
                            ins = pe.matmul(tok_ps[:, t, :], hT[:, k, t * T:(t + 1) * T], w2[:, k, :],
                                            start=(k == 0), stop=(k == KH - 1))
                    ins.then_inc(s_tok2, 1)

                def turn_and_v(g):
                    pe.wait_ge(s_xtok, g * NT + NT)
                    wait(pe, s_x2a, g * 2)
                    wait(pe, s_x2d, g * 2)
                    for t in range(NT):
                        pe.transpose(B[2][:, t * T:(t + 1) * T], xtok[:, t, 0:DM], ident[0:T, 0:T])
                    for t in range(NT):
                        ins = pe.transpose(B[3][0:DR, t * T:(t + 1) * T], xtok[:, t, DM:D], ident[0:T, 0:T])
                    ins.then_inc(s_x2ps, 1)
                    pe.wait_ge(s_x2a, g * 2 + 2)
                    pe.wait_ge(s_x2d, g * 2 + 2)
                    for t in range(NT):
                        for c in range(3):
                            i = 3 * t + c
                            wait(pe, s_vsb, g * 9 + (i - 1 if i else 0))
                            o = B[4 + i % 2][0:T, :]
                            cs = slice(c * 512, (c + 1) * 512)
                            ts = slice(t * T, (t + 1) * T)
                            in_parts(pe, o, (x2gh[:, ts], x2gl[:, ts], x2gs[:, ts]),
                                     (wvh[:, cs], wvl[:, cs], wvhh[:, cs], wvrl[:, cs]), True, True).then_inc(s_v, 1)

                tok1(0)
                pe.wait_ge(s_w2, 16)
                pe.wait_ge(s_id, 2)
                tok2(0)
                tok1(1)
                pe.wait_ge(s_vlo, 2)
                turn_and_v(0)
                with pe.Fori(1, NG - 1) as g:
                    tok2(g)
                    tok1(g + 1)
                    turn_and_v(g)
                tok2(NG - 1)
                turn_and_v(NG - 1)

            @block.scalar
            def _(act):
                def hidden(g, m):
                    act.wait_ge(s_tok1, g * KH + m + 1)
                    act.activation(hT[:, m, :], B[m % 2][:, 0:G], ACT.Relu, bias=b1s[:, m:m + 1]).then_inc(s_hT, 1)

                def root(g):
                    act.wait_ge(s_var, g + 1)
                    act.activation(std[:, :], ve[:, :], ACT.Sqrt).then_inc(s_std, 1)

                def turned(g):
                    act.wait_ge(s_x2ps, g + 1)
                    wait(act, s_x2T, g * 3)
                    act.activation(x2gh[:, :], B[2][:, 0:G], ACT.Copy).then_inc(s_x2a, 1)
                    act.activation(x2gs[0:DR, :], B[3][0:DR, 0:G], ACT.Copy).then_inc(s_x2a, 1)

                def x_high(g, halves=(0, 1)):
                    for c in halves:
                        ks = slice(c * XC, (c + 1) * XC)
                        if isinstance(g, int) and g == 0 and c == 0:
                            act.wait_ge(s_x0, 16)
                        else:
                            act.wait_ge(s_x, 16 * g + 16)
                        act.activation(xh[:, ks, :], xraw[:, ks, :], ACT.Copy).then_inc(s_xh, 1)

                def w1_high(m):
                    act.wait_ge(s_w1[m], 16)
                    act.activation(w1h[:, m, :, :], w1[:, m, :, :], ACT.Copy).then_inc(s_w1h, 1)

                def turn(g):
                    hidden(g + 1, 0)
                    root(g)
                    for m in range(1, KH):
                        hidden(g + 1, m)
                        if m == 3:
                            high_parts(act, g, qk_parts, g)
                    turned(g)

                x_high(0, (0,))
                w1_high(0)
                x_high(0, (1,))
                w1_high(1)
                act.wait_ge(s_small, 16)
                for m in range(KH):
                    hidden(0, m)
                    if m + 2 < KH:
                        w1_high(m + 2)
                x_high(1)
                act.wait_ge(s_rawv, 48)
                act.activation(wvh[:, :], vtok[:, 0, :], ACT.Copy).then_inc(s_vhi, 1)
                act.activation(wvhh[:, :], vtok[:, 1, :], ACT.Copy).then_inc(s_vhi, 1)
                with act.Fori(0, NG - 2) as g:
                    turn(g)
                    x_high(g + 2)
                turn(NG - 2)
                high_parts(act, NG - 1, qk_parts, NG - 1)
                root(NG - 1)
                turned(NG - 1)

            @block.vector
            def _(dve):
                link = Chain(dve, s_dve)
                for m in range(KH):
                    if m < 2:
                        ks = slice(m * XC, (m + 1) * XC)
                        dve.wait_ge(s_xh, m + 1)
                        dve.tensor_tensor(xl[:, ks, :], xraw[:, ks, :], xh[:, ks, :].bitcast(F32),
                                          ALU.subtract).then_inc(s_xl0, 1)
                    dve.wait_ge(s_w1h, m + 1)
                    dve.tensor_tensor(w1l[:, m, :, :], w1[:, m, :, :], w1h[:, m, :, :].bitcast(F32),
                                      ALU.subtract).then_inc(s_w1l, 1)
                dve.wait_ge(s_smalld, 32)

                def group(g):
                    link.loop(g, LN_LINKS + 1)
                    dve.wait_ge(s_tok2, g + 1)
                    wait(dve, s_x2ps, g)
                    dve.tensor_tensor(hsum[:, :, :], tok_ps, b2s[:, None, :].broadcast_to([T, NT, D]),
                                      ALU.add).then_inc(s_hsum, 1)
                    dve.wait_ge(s_hsum, g + 1)
                    link(dve.tensor_scalar(h_all[:, ds(g * NT, NT), :], hsum[:, :, :], 0.0, None, ALU.max))

                    layer_norm(dve, link, lambda t: h_all[:, ds(g * NT + t, 1), :].rearrange("p a d -> p (a d)"),
                               ln, g, s_var, s_std, s_xtok, spare)
                    if isinstance(g, int):
                        dve.wait_ge(s_vhi, 1)
                        dve.tensor_tensor(wvl[:, :], vtok[:, 0, :], wvh[:, :].bitcast(F32), ALU.subtract).then_inc(s_vlo, 1)
                        dve.wait_ge(s_vhi, 2)
                        dve.tensor_tensor(wvrl[:, :], vtok[0:DR, 1, :], wvhh[0:DR, :].bitcast(F32),
                                          ALU.subtract).then_inc(s_vlo, 1)
                    dve.wait_ge(s_x2a, g * 2 + 1)
                    dve.tensor_tensor(x2gl[:, :], B[2][:, 0:G], x2gh[:, :].bitcast(F32),
                                      ALU.subtract).then_inc(s_x2d, 1)
                    dve.wait_ge(s_x2a, g * 2 + 2)
                    dve.tensor_tensor(x2gs[DR:128, :], B[3][0:DR, 0:G], x2gs[0:DR, :].bitcast(F32),
                                      ALU.subtract).then_inc(s_x2d, 1)
                    for t in range(NT):
                        wait(dve, s_vout[t], g * 16)
                        for c in range(3):
                            i = 3 * t + c
                            cs = slice(c * 512, (c + 1) * 512)
                            dve.wait_ge(s_v, g * 9 + i + 1)
                            dve.tensor_tensor(vtok[0:T, t, cs], B[4 + i % 2][0:T, :], bvs[:, cs],
                                              ALU.add).then_inc(s_vsb, 1)
                    link.end()

                group(0)
                with dve.Fori(1, NG) as g:
                    group(g)

        s_qk = sem("s_qk")
        s_proj = sem("s_proj")
        s_hsum = sem("s_hsum2")
        s_var = sem("s_var2")
        s_std = sem("s_std2")
        s_xtok = sem("s_xtok2")
        s_dve = sem("s_dve2")
        ln["s_stat"] = sem("s_stat2")
        proj_ps = [B[1][0:T, 0:D], B[1][0:T, 256:256 + D], B[0][0:T, 0:D]]


        def items(g):
            return g * RING - 2 if not isinstance(g, int) or g > 0 else 0

        def close(dve, link, g):
            link.loop(g, LN_LINKS + 1)
            dve.wait_ge(s_proj, g + 1)
            if not isinstance(g, int) or g > 0:
                dve.wait_ge(s_qk, items(g) + RING)
                dve.wait_ge(s_x3out, g * NT * 16)
            dve.tensor_tensor(hsum[:, 0:2, :], B[1][0:T, 0:512].rearrange("p (t c) -> p t c", t=2)[:, :, 0:D],
                              bps[:, None, :].broadcast_to([T, 2, D]), ALU.add)
            dve.tensor_tensor(hsum[:, 2, :], proj_ps[2], bps[:, :], ALU.add).then_inc(s_hsum, 1)
            dve.wait_ge(s_hsum, g + 1)
            hg = h_all[:, ds(g * NT, NT), :]
            link(dve.tensor_tensor(hg, hg, hsum[:, :, :], ALU.add))

            layer_norm(dve, link, lambda t: h_all[:, ds(g * NT + t, 1), :].rearrange("p a d -> p (a d)"),
                       ln, g, s_var, s_std, s_xtok, spare)
            link.end()

        with ExitStack() as st:
            def sb(name, shape, dt=F32):
                return st.enter_context(nc.sbuf_tensor(name, shape, dt))

            def sem(name):
                return st.enter_context(nc.semaphore(name))

            qm = sb("qm", [DM, G, HEADS])
            qr = sb("qr", [DR, G, HEADS])
            km = sb("km", [DM, G, HEADS])
            kr = sb("kr", [DR, G, HEADS])
            vp = sb("vp", [PAIR, NB * BP, D])
            ph = sb("ph", [DM, QKV], F32R)
            pl = sb("pl", [DM, QKV], F32R)
            phh = sb("phh", [128, QKV], F32R)
            prl = sb("prl", [DR, QKV], F32R)
            proj_parts = (ph, pl, phh, prl)
            oh = sb("oh", [DM, G, HEADS], F32R)
            ol = sb("ol", [DM, G, HEADS], F32R)
            os_ = sb("os", [128, G, HEADS], F32R)
            oraw = sb("oraw", [128, 2, BW])
            pr = sb("pr", [PAIR, 4, BP, PAIR])
            pt = sb("pt", [PAIR, 2, BW])
            mx = sb("mx", [PAIR, 4, BP])
            sm = sb("sm", [PAIR, 4, BP])
            ri = sb("ri", [PAIR, 4, BP])
            blkb = sb("blkb", [2, 2 * PAIR], BF16)

            s_blk = sem("s_blk")
            s_qka = sem("s_qka")
            s_qkd = sem("s_qkd")
            s_vin = sem("s_vin")
            s_e = sem("s_e")
            s_max = sem("s_max")
            s_sub = sem("s_sub")
            s_exp = sem("s_exp")
            s_sum = sem("s_sum")
            s_rec = sem("s_rec")
            s_prob = sem("s_prob")
            s_at = sem("s_at")
            s_atsb = sem("s_atsb")
            s_o = sem("s_o")
            s_oh = sem("s_oh")
            s_ol = sem("s_ol")
            block = st.enter_context(nc.Block())

            def evacuated(who, g, i):
                before = g * owned(who, RING) - 1 if not isinstance(g, int) or g > 0 else 0
                return before + owned(who, i)

            def bank(i):
                return B[RING_BANKS[i % 4]]

            @block.sync
            def _(sp):
                def load_v(g):
                    wait(sp, s_o, g * NB)
                    sp.dma_start(vp[:, :, :], v_dram[ds(g * G, G), :].rearrange(
                        "(n t) (j d) -> (t j) n d", t=9, j=HEADS)).then_inc(s_vin, 16)

                def store_x3(g):
                    sp.wait_ge(s_xtok, g * NT + NT)
                    for t in range(NT):
                        sp.dma_start(x3_dram[ds(g * G + t * T, T), :], xtok[:, t, :]).then_inc(s_x3out, 16)

                load_raw(sp, NQC)
                load_v(0)
                load_raw(sp, NQC + 1)
                with sp.Fori(0, NG - 1) as g:
                    store_x3(g)
                    load_v(g + 1)

            @block.tensor
            def _(pe):
                def ring_free(g, i):
                    if i >= 4:
                        who = OWNER[i - 4]
                        pe.wait_ge(s_qka if who == "A" else s_qkd, evacuated(who, g, i - 3))

                def x3_turn(g, at):
                    pe.wait_ge(s_xtok, g * NT + NT)
                    ring_free(g + 1, at)
                    ring_free(g + 1, at + 1)
                    for t in range(NT):
                        ins = pe.transpose(bank(at)[:, t * T:(t + 1) * T], xtok[:, t, 0:DM], ident[0:T, 0:T])
                    ins.then_inc(s_qk, 1)
                    for t in range(NT):
                        ins = pe.transpose(bank(at + 1)[0:DR, t * T:(t + 1) * T], xtok[:, t, DM:D], ident[0:T, 0:T])
                    ins.then_inc(s_qk, 1)

                def scores(g, b):
                    if b >= NSB:
                        pe.wait_ge(s_sub, g * NB + b - NSB + 1)
                    for p in range(BP):
                        o = B[SCORE_BANKS[b % NSB]][0:PAIR, p * PAIR:(p + 1) * PAIR]
                        ts = slice((b * BP + p) * 9, (b * BP + p + 1) * 9)
                        pe.matmul(o, blkb[:, 0:PAIR], blkb[:, PAIR:2 * PAIR], start=True, stop=False)
                        pe.matmul(o, qm[:, ts, :].rearrange("p t j -> p (t j)"),
                                  km[:, ts, :].rearrange("p t j -> p (t j)"), start=False, stop=False)
                        ins = pe.matmul(o, qr[:, ts, :].rearrange("p t j -> p (t j)"),
                                        kr[:, ts, :].rearrange("p t j -> p (t j)"), start=False, stop=True)
                    ins.then_inc(s_e, 1)

                def turn_probs(g, b):
                    pe.wait_ge(s_prob, g * NB + b + 1)
                    if not isinstance(g, int) or g or b >= 2:
                        pe.wait_ge(s_atsb, g * NB + b - 1)
                    for p in range(BP):
                        ins = pe.transpose(B[4 + b % 2][0:PAIR, p * PAIR:(p + 1) * PAIR], pr[:, b % 4, p, :],
                                           ident[0:PAIR, 0:PAIR])
                    ins.then_inc(s_at, 1)

                def weigh(g, b):
                    pe.wait_ge(s_atsb, g * NB + b + 1)
                    if not isinstance(g, int) or g or b:
                        pe.wait_ge(s_oh, 4 * (g * NB + b))
                    for p in range(BP):
                        cs = slice(p * PAIR, (p + 1) * PAIR)
                        pe.matmul(B[6][:, cs], vp[:, b * BP + p, 0:DM], pt[:, b % 2, cs], start=True, stop=True)
                        ins = pe.matmul(B[7][0:DR, cs], vp[:, b * BP + p, DM:D], pt[:, b % 2, cs],
                                        start=True, stop=True)
                    ins.then_inc(s_o, 1)

                def project(g, t, batches, j0, j1):
                    pe.wait_ge(s_ol, 2 * (g * NB + batches))
                    ts = slice(t * T, (t + 1) * T)
                    for j in range(j0, j1):
                        cs = slice(j * D, (j + 1) * D)
                        ins = in_parts(pe, proj_ps[t], (oh[:, ts, j], ol[:, ts, j], os_[:, ts, j]),
                                       (ph[:, cs], pl[:, cs], phh[:, cs], prl[:, cs]), j == 0, j == HEADS - 1)
                    return ins

                def group(g):
                    first = isinstance(g, int)
                    for i in range(NQK):
                        ring_free(g, i)
                        cs, ts = slice(i * 128, (i + 1) * 128), ds(g * G, G)
                        in_parts(pe, bank(i)[:, 0:G], (x2h[:, ts], x2l[:, ts], x2s[:, ts]),
                                 (wh[:, cs], wl[:, cs], whh[:, cs], wrl[:, cs]), True, True, w_stationary=True).then_inc(s_qk, 1)
                    if not first:
                        x3_turn(g - 1, NQK)
                    last = NQK if first else RING
                    pe.wait_ge(s_qka, evacuated("A", g, last))
                    pe.wait_ge(s_qkd, evacuated("D", g, last))
                    pe.wait_ge(s_vin, g * 16 + 16)
                    for b in range(AHEAD):
                        scores(g, b)
                    for b in range(NB):
                        if b == 1 and not first:
                            pe.wait_ge(s_hsum, g)
                        if b + AHEAD < NB:
                            scores(g, b + AHEAD)
                        if b == 1 and not first:
                            logits(pe, B[1][:, 0:G], ds((g - 1) * G, G)).then_inc(s_rps, 1)
                        if b == NB - 2:
                            if first:
                                pe.wait_ge(s_spm, NQC + 2)
                                pe.wait_ge(s_spr, NQC + 2)
                            else:
                                pe.wait_ge(s_sc, g)
                            project(g, 0, 3, 0, HEADS // 2)
                        if b == NB - 1:
                            project(g, 0, 3, HEADS // 2, HEADS)
                        turn_probs(g, b)
                        if b >= 1:
                            weigh(g, b - 1)
                    project(g, 1, 6, 0, HEADS // 2)
                    weigh(g, NB - 1)
                    project(g, 1, 6, HEADS // 2, HEADS)
                    project(g, 2, NB, 0, HEADS).then_inc(s_proj, 1)

                pe.wait_ge(s_watt, 5 * 16)
                pe.wait_ge(s_blk, 1)
                group(0)
                with pe.Fori(1, NG) as g:
                    group(g)

            def part(o, b):
                return o[:, b * 36:(b + 1) * 36, :].rearrange("p t j -> p (t j)")

            def ring_item(eng, g, i, evac):
                eng.wait_ge(s_qk, items(g) + i + 1)
                m, r = (qm, qr) if i < NQK // 2 else (km, kr)
                p, w = (i % 12) // 3, i % 3
                wait(eng, s_e, g * NB)
                if w > 0:
                    return evac(m[:, :, 2 * p + w - 1], bank(i)[:, 0:G], bqks[:, i:i + 1])
                evac(r[:, :, 2 * p], bank(i)[0:DR, 0:G], bqks[0:DR, i:i + 1])
                return evac(r[:, :, 2 * p + 1], bank(i)[DR:128, 0:G], bqks[DR:128, i:i + 1])

            @block.scalar
            def _(act):
                def evac(o, i, bias):
                    return act.activation(o, i, ACT.Identity, bias=bias)

                def root(g):
                    act.wait_ge(s_var, g + 1)
                    act.activation(std[:, :], ve[:, :], ACT.Sqrt).then_inc(s_std, 1)

                def x3_main(g, at):
                    act.wait_ge(s_qk, items(g + 1) + at + 1)
                    act.activation(x3Tm[:, ds(g * G, G)], bank(at)[:, 0:G], ACT.Copy).then_inc(s_qka, 1)

                def exps(g, b):
                    act.wait_ge(s_sub, g * NB + b + 1)
                    act.activation(pr[:, b % 4, :, :], pr[:, b % 4, :, :], ACT.Exp).then_inc(s_exp, 1)

                def output(g, b):
                    act.wait_ge(s_o, g * NB + b + 1)
                    if not isinstance(g, int):
                        act.wait_ge(s_proj, g)
                    if not isinstance(g, int) or b > 0:
                        act.wait_ge(s_ol, 2 * (g * NB + b))
                    act.activation(oraw[:, 0, :], B[6][:, 0:BW], ACT.Copy).then_inc(s_oh, 1)
                    act.activation(part(oh, b), B[6][:, 0:BW], ACT.Copy).then_inc(s_oh, 1)
                    act.activation(oraw[0:DR, 1, :], B[7][0:DR, 0:BW], ACT.Copy).then_inc(s_oh, 1)
                    act.activation(part(os_, b)[0:DR], B[7][0:DR, 0:BW], ACT.Copy).then_inc(s_oh, 1)

                def group(g):
                    for i in range(NQK):
                        if OWNER[i] == "A":
                            ring_item(act, g, i, evac).then_inc(s_qka, 1)
                        if i == 3 and not isinstance(g, int):
                            root(g - 1)
                    if not isinstance(g, int):
                        x3_main(g - 1, NQK)
                    for b in range(AHEAD):
                        exps(g, b)
                    if isinstance(g, int):
                        high_parts(act, NQC, proj_parts, 0)
                    for b in range(NB):
                        act.wait_ge(s_at, g * NB + b + 1)
                        if not isinstance(g, int) or b >= 2:
                            act.wait_ge(s_o, g * NB + b - 1)
                        act.activation(pt[:, b % 2, :], B[4 + b % 2][0:PAIR, 0:BW], ACT.Copy,
                                       scale=float(D) ** -0.5).then_inc(s_atsb, 1)
                        if b + AHEAD < NB:
                            exps(g, b + AHEAD)
                        if b >= 1:
                            output(g, b - 1)
                        if b == 2 and isinstance(g, int):
                            high_parts(act, NQC + 1, proj_parts, 1)
                        if b == 1 and not isinstance(g, int):
                            act.wait_ge(s_rps, g)
                            act.activation(sel[:, ds((g - 1) * G, G)], B[1][0:E, 0:G], ACT.Sigmoid).then_inc(s_sc, 1)
                    output(g, NB - 1)

                group(0)
                with act.Fori(1, NG) as g:
                    group(g)

            @block.gpsimd
            def _(pool):
                def normalise(g, b):
                    pool.wait_ge(s_rec, g * NB + b + 1)
                    pool.tensor_tensor(pr[:, b % 4, :, :], pr[:, b % 4, :, :],
                                       ri[:, b % 4, :].unsqueeze(2).broadcast_to([PAIR, BP, PAIR]),
                                       ALU.mult).then_inc(s_prob, 1)

                def output_low(g, b):
                    pool.wait_ge(s_oh, 4 * (g * NB + b) + 2)
                    pool.tensor_tensor(part(ol, b), oraw[:, 0, :], part(oh, b).bitcast(F32),
                                       ALU.subtract).then_inc(s_ol, 1)
                    pool.wait_ge(s_oh, 4 * (g * NB + b) + 4)
                    pool.wait_ge(s_ol, 2 * (g * NB + b) + 1)
                    pool.tensor_tensor(part(os_, b)[DR:128], oraw[0:DR, 1, :],
                                       part(os_, b)[0:DR].bitcast(F32), ALU.subtract).then_inc(s_ol, 1)
                    pool.wait_ge(s_ol, 2 * (g * NB + b) + 2)

                lows = {1: (low_main, 0), 2: (low_rest, 0), 3: (low_main, 1), 4: (low_rest, 1)}
                for b in range(NB):
                    normalise(0, b)
                    if b >= 3:
                        output_low(0, b - 3)
                    if b in lows:
                        low, c = lows[b]
                        low(pool, NQC + c, proj_parts, c)
                for b in range(NB - 3, NB):
                    output_low(0, b)
                with pool.Fori(1, NG) as g:
                    for b in range(NB):
                        normalise(g, b)
                        if b >= 3:
                            output_low(g, b - 3)
                    for b in range(NB - 3, NB):
                        output_low(g, b)

            @block.vector
            def _(dve):
                link = Chain(dve, s_dve)

                def evac(o, i, bias):
                    return dve.tensor_scalar(o, i, bias, None, ALU.add)

                def x3_rest(g, at):
                    dve.wait_ge(s_qk, items(g + 1) + at + 2)
                    dve.tensor_copy(x3Tr[:, ds(g * G, G)], bank(at + 1)[0:DR, 0:G]).then_inc(s_qkd, 1)

                def centre(g, b):
                    sc = B[SCORE_BANKS[b % NSB]][0:PAIR, 0:BW].rearrange("p (n k) -> p n k", n=BP)
                    dve.wait_ge(s_e, g * NB + b + 1)
                    dve.tensor_reduce(mx[:, b % 4, :], sc, AX.X, ALU.max).then_inc(s_max, 1)
                    dve.wait_ge(s_max, g * NB + b + 1)
                    if not isinstance(g, int) or g > 0 or b >= 4:
                        dve.wait_ge(s_at, g * NB + b - 3)
                    dve.tensor_tensor(pr[:, b % 4, :, :], sc,
                                      mx[:, b % 4, :].unsqueeze(2).broadcast_to([PAIR, BP, PAIR]),
                                      ALU.subtract).then_inc(s_sub, 1)

                def sums(g, b):
                    dve.wait_ge(s_exp, g * NB + b + 1)
                    dve.tensor_reduce(sm[:, b % 4, :], pr[:, b % 4, :, :], AX.X, ALU.add).then_inc(s_sum, 1)
                    dve.wait_ge(s_sum, g * NB + b + 1)
                    if not isinstance(g, int) or g > 0 or b >= 4:
                        dve.wait_ge(s_prob, g * NB + b - 3)
                    dve.reciprocal(ri[:, b % 4, :], sm[:, b % 4, :]).then_inc(s_rec, 1)

                def group(g, picks):
                    for i in range(NQK):
                        if OWNER[i] == "D":
                            ring_item(dve, g, i, evac).then_inc(s_qkd, 1)
                    if not isinstance(g, int) or g > 0:
                        x3_rest(g - 1, NQK)
                    for b in range(AHEAD):
                        centre(g, b)
                        sums(g, b)
                    for b in range(NB):
                        if b + AHEAD < NB:
                            centre(g, b + AHEAD)
                            sums(g, b + AHEAD)
                        if picks[b]:
                            dve.wait_ge(s_sc, 2)
                            first_picks.steps(picks[b])

                dve.tensor_copy(blkb[:, :], blk[:, :]).then_inc(s_blk, 1)
                first_picks = Pick(dve, scA, topsA, topiA, s_topA)
                rounds = [[0] * NB, [0] * NB, PICKS_2, PICKS_3]
                for g in range(NG):
                    if g:
                        close(dve, link, g - 1)
                    group(g, rounds[g])

        attn.close()

        with ExitStack() as st:
            def sb(name, shape, dt=F32):
                return st.enter_context(nc.sbuf_tensor(name, shape, dt))

            def sem(name):
                return st.enter_context(nc.semaphore(name))

            wsm = sb("wsm", [DM, 2 * F_SH])
            wsr = sb("wsr", [DR, 2 * F_SH])
            wsd = sb("wsd", [128, KS, D])
            sgate = sb("sgate", [128, KS, G])
            sup = sb("sup", [128, KS, G])
            sa = sb("sa", [128, KS, G])
            ysh = sb("ysh", [T, NT, D])
            second = sb("second", [DR + E, NA + 2 * CAP])[DR:]
            scB, topsB, topiB = second[:, 0:NA], second[:, NA:NA + CAP], second[:, NA + CAP:].bitcast(U32)
            idA = sb("idA", [DR + E, CAP])[DR:]
            idB = sb("idB", [DR + E, CAP])[DR:]
            isB = sb("isB", [DR + E, CAP])[DR:]
            diff = sb("diff", [DR + E, CAP])[DR:]
            tops = sb("tops", [E, CAP])
            topf = sb("topf", [E, CAP])
            idx = sb("idx", [HC, 2, E], U32)
            scr = sb("scr", [HC, 2, E])
            idg = sb("idg", [HC, 2, 2], U32)
            ids = sb("ids", [HC, 2, 2], U32)
            wgm = [sb(f"wgm{u}", [DM, 2 * F_EXP]) for u in range(2)]
            wgr = [sb(f"wgr{u}", [DR, 2 * F_EXP]) for u in range(2)]
            wd = [sb(f"wd{u}", [128, KF, D]) for u in range(2)]
            xg = [sb(f"xg{u}", [HC, 2, D]) for u in range(2)]
            xgm = [sb(f"xgm{u}", [DM, CAP]) for u in range(2)]
            xgr = [sb(f"xgr{u}", [DR, CAP]) for u in range(2)]
            sl = sb("sl", [128, 2, 2, CAP])
            act32 = sb("act32", [128, 2, 2, CAP])
            ah = [sb(f"ah{u}", [128, KF, CAP], F32R) for u in range(2)]
            al = [sb(f"al{u}", [128, KF, CAP], F32R) for u in range(2)]
            wdh = [sb(f"wdh{u}", [128, KF, D], F32R) for u in range(2)]
            wdl = [sb(f"wdl{u}", [128, KF, D], F32R) for u in range(2)]
            ys = [sb(f"ys{u}", [HC, 2, D]) for u in range(2)]

            s_ws = sem("s_ws")
            s_wsd = sem("s_wsd")
            s_x3ps = sem("s_x3ps")
            s_x3a = sem("s_x3a")
            s_x3d = sem("s_x3d")
            s_top = sem("s_top")
            s_topT = sem("s_topT")
            s_pick = sem("s_pick")
            s_idx = sem("s_idx")
            s_sg = sem("s_sg")
            s_sga = sem("s_sga")
            s_sa = sem("s_sa")
            s_sd = sem("s_sd")
            s_sda = sem("s_sda")
            s_ysh = sem("s_ysh")
            s_init = sem("s_init")
            s_wgu = [sem(f"s_wgu{u}") for u in range(2)]
            s_wd = [sem(f"s_wd{u}") for u in range(2)]
            s_idg = sem("s_idg")
            s_ids = sem("s_ids")
            s_gath = [sem(f"s_gath{u}") for u in range(2)]
            s_xgt = sem("s_xgt")
            s_xga = sem("s_xga")
            s_xgd = sem("s_xgd")
            s_gu = sem("s_gu")
            s_silu = sem("s_silu")
            s_prod = sem("s_prod")
            s_ah = sem("s_ah")
            s_act = sem("s_act")
            s_wdh = sem("s_wdh")
            s_wdl = sem("s_wdl")
            s_y = sem("s_y")
            s_ys = sem("s_ys")
            s_scat = sem("s_scat")
            s_carry = sem("s_carry")
            block = st.enter_context(nc.Block())

            gu_banks = [(2, 3), (4, 5), (0, 1)]
            ysh_ps = [B[6][0:T, 0:D], B[6][0:T, 256:256 + D], B[7][0:T, 0:D]]
            ITEMS = KF // 2

            @block.sync
            def _(sp):
                sp.dma_start(wsm[:, :], Wsgu[0:DM, :]).then_inc(s_ws, 16)
                sp.dma_start(wsr[:, :], Wsgu[DM:D, :]).then_inc(s_ws, 16)
                sp.dma_start(wsd[:, :, :], Wsd).then_inc(s_wsd, 16)

                def load_gu(e, u):
                    sp.dma_start(wgm[u][:, :], Wgu[ds(e, 1), 0:DM, :].rearrange("a p f -> (a p) f")).then_inc(s_wgu[u], 16)
                    sp.dma_start(wgr[u][:, :], Wgu[ds(e, 1), DM:D, :].rearrange("a p f -> (a p) f")).then_inc(s_wgu[u], 16)

                def load_d(e, u):
                    sp.dma_start(wd[u][:, :, :], Wd[ds(e, 1)].rearrange("a p k d -> (a p) k d")).then_inc(s_wd[u], 16)

                for e in range(2):
                    load_gu(e, e)
                    load_d(e, e)
                sp.wait_ge(s_xtok, NG * NT)
                for t in range(NT):
                    sp.dma_start(x3_dram[N - G + t * T:N - G + (t + 1) * T, :], xtok[:, t, :]).then_inc(s_x3out, 16)
                with sp.Fori(0, NG) as g:
                    sp.wait_ge(s_ysh, g + 1)
                    for t in range(NT):
                        sp.dma_start(out_rows[ds(g * G + t * T, T), :], ysh[:, t, :]).then_inc(s_init, 16)
                with sp.Fori(1, E // 2) as i:
                    for u in range(2):
                        e = 2 * i + u
                        sp.wait_ge(s_gu, (e - 2) * ITEMS + ITEMS)
                        load_gu(e, u)
                        sp.wait_ge(s_wdl, e - 1)
                        load_d(e, u)

            @block.tensor
            def _(pe):
                def gate_up_sh(g, m):
                    xm, xr = x3Tm[:, ds(g * G, G)], x3Tr[:, ds(g * G, G)]
                    if not isinstance(g, int) or g > 0:
                        pe.wait_ge(s_sga, (g - 1) * KS + m + 1)
                    for w in range(2):
                        o = B[gu_banks[m][w]][:, 0:G]
                        fs = slice(w * F_SH + m * 128, w * F_SH + (m + 1) * 128)
                        pe.matmul(o, wsm[:, fs], xm, start=True, stop=False)
                        ins = pe.matmul(o, wsr[:, fs], xr, start=False, stop=True)
                    ins.then_inc(s_sg, 1)

                def down_sh(g):
                    pe.wait_ge(s_sa, g * KS + KS)
                    wait(pe, s_sda, g * NT)
                    for t in range(NT):
                        for k in range(KS):
                            ins = pe.matmul(ysh_ps[t], sa[:, k, t * T:(t + 1) * T], wsd[:, k, :],
                                            start=(k == 0), stop=(k == KS - 1))
                    ins.then_inc(s_sd, 1)

                pe.wait_ge(s_ws, 2 * 16)
                gate_up_sh(0, 0)
                pe.wait_ge(s_xtok, NG * NT)
                for t in range(NT):
                    pe.transpose(B[6][:, t * T:(t + 1) * T], xtok[:, t, 0:DM], ident[0:T, 0:T])
                for t in range(NT):
                    ins = pe.transpose(B[7][0:DR, t * T:(t + 1) * T], xtok[:, t, DM:D], ident[0:T, 0:T])
                ins.then_inc(s_x3ps, 1)
                gate_up_sh(0, 1)
                pe.wait_ge(s_x3a, 1)
                pe.wait_ge(s_x3d, 1)
                logits(pe, B[6][:, 0:G], slice(N - G, N)).then_inc(s_rps, 1)
                pe.wait_ge(s_hsum, NG)
                gate_up_sh(0, 2)
                gate_up_sh(1, 0)
                pe.wait_ge(s_sc, NG + 1)
                pe.wait_ge(s_wsd, 16)
                down_sh(0)
                gate_up_sh(1, 1)
                gate_up_sh(1, 2)
                with pe.Fori(1, NG - 1) as g:
                    gate_up_sh(g + 1, 0)
                    down_sh(g)
                    gate_up_sh(g + 1, 1)
                    gate_up_sh(g + 1, 2)
                down_sh(NG - 1)
                pe.wait_ge(s_sda, NG * NT)
                pe.wait_ge(s_pick, 6)
                for n in range(2):
                    for h in range(2):
                        src = (topf, tops)[n]
                        ins = pe.transpose(B[5][0:HC, (2 * n + h) * E:(2 * n + h + 1) * E],
                                           src[:, h * HC:(h + 1) * HC], ident[0:E, 0:E])
                ins.then_inc(s_topT, 1)
                pe.wait_ge(s_idx, 2)

                def turn_tokens(i, u):
                    e = 2 * i + u
                    pe.wait_ge(s_gath[u], 32 * i + 32)
                    wait(pe, s_xga, e)
                    wait(pe, s_xgd, e)
                    for h in range(2):
                        pe.transpose(B[5][:, h * HC:(h + 1) * HC], xg[u][:, h, 0:DM], ident[0:HC, 0:HC])
                        ins = pe.transpose(B[4][0:DR, h * HC:(h + 1) * HC], xg[u][:, h, DM:D],
                                           ident[0:HC, 0:HC])
                    ins.then_inc(s_xgt, 1)

                def gate_up(e, u, n):
                    r = (ITEMS * u + n) % 2
                    if not isinstance(e, int) or e * ITEMS + n >= 2:
                        pe.wait_ge(s_prod, e * ITEMS + n - 1)
                    for w in range(2):
                        for m in range(2):
                            o = B[2 * w + r][:, m * CAP:(m + 1) * CAP]
                            f = w * F_EXP + (2 * n + m) * 128
                            pe.matmul(o, wgm[u][:, f:f + 128], xgm[u][:, :], start=True, stop=False)
                            ins = pe.matmul(o, wgr[u][:, f:f + 128], xgr[u][:, :], start=False, stop=True)
                    ins.then_inc(s_gu, 1)

                def down(i, u):
                    e = 2 * i + u
                    pe.wait_ge(s_wdl, e + 1)
                    pe.wait_ge(s_act, e * ITEMS + ITEMS - 1)
                    if not isinstance(e, int) or e >= 2:
                        pe.wait_ge(s_ys, 2 * e - 2)
                    for h in range(2):
                        parts = [(a, w, k) for k in range(KF) for a, w in
                                 ((ah[u], wdh[u]), (ah[u], wdl[u]), (al[u], wdh[u]))]
                        for n, (a, w, k) in enumerate(parts):
                            if h == 0 and n == len(parts) * (ITEMS - 1) // ITEMS:
                                pe.wait_ge(s_act, e * ITEMS + ITEMS)
                            ins = pe.matmul(B[6 + u][0:HC, h * 256:h * 256 + D], a[:, k, h * HC:(h + 1) * HC],
                                            w[:, k, :], start=(n == 0), stop=(n == len(parts) - 1))
                    ins.then_inc(s_y, 1)

                def turn(i, u):
                    e = 2 * i + u
                    pe.wait_ge(s_xga, e + 1)
                    pe.wait_ge(s_xgd, e + 1)
                    pe.wait_ge(s_wgu[u], 32 * i + 32)
                    gate_up(e, u, 0)
                    if not isinstance(e, int) or e > 0:
                        down(*((i, 0) if u else (i - 1, 1)))
                    gate_up(e, u, 1)
                    if not isinstance(e, int) or e < E - 1:
                        turn_tokens(*((i + 1, 0) if u else (i, 1)))
                    gate_up(e, u, 2)

                turn_tokens(0, 0)
                turn(0, 0)
                turn(0, 1)
                with pe.Fori(1, E // 2 - 1) as i:
                    turn(i, 0)
                    turn(i, 1)
                turn(E // 2 - 1, 0)
                turn(E // 2 - 1, 1)
                down(E // 2 - 1, 1)

            @block.scalar
            def _(act):
                act.activation(scB[:, 0:G], sel[:, N // 2:N // 2 + G], ACT.Copy).then_inc(s_sc, 1)

                def item(g, m):
                    act.wait_ge(s_sg, g * KS + m + 1)
                    if not isinstance(g, int) or g > 0:
                        act.wait_ge(s_sa, (g - 1) * KS + m + 1)
                    act.activation(sgate[:, m, :], B[gu_banks[m][0]][:, 0:G], ACT.Silu)
                    act.activation(sup[:, m, :], B[gu_banks[m][1]][:, 0:G], ACT.Copy).then_inc(s_sga, 1)

                def output_sh(g):
                    act.wait_ge(s_sd, g + 1)
                    wait(act, s_init, g * NT * 16)
                    for t in range(NT):
                        act.activation(ysh[:, t, :], ysh_ps[t], ACT.Copy).then_inc(s_sda, 1)

                act.wait_ge(s_var, NG)
                act.activation(std[:, :], ve[:, :], ACT.Sqrt).then_inc(s_std, 1)
                item(0, 0)
                act.wait_ge(s_x3ps, 1)
                act.activation(x3Tm[:, N - G:N], B[6][:, 0:G], ACT.Copy).then_inc(s_x3a, 1)
                item(0, 1)
                act.wait_ge(s_rps, NG)
                act.activation(scB[:, G:2 * G], B[6][0:E, 0:G], ACT.Sigmoid).then_inc(s_sc, 1)
                item(0, 2)
                item(1, 0)
                output_sh(0)
                item(1, 1)
                item(1, 2)
                with act.Fori(1, NG - 1) as g:
                    item(g + 1, 0)
                    output_sh(g)
                    item(g + 1, 1)
                    item(g + 1, 2)
                output_sh(NG - 1)

                def tokens_main(e, u):
                    act.wait_ge(s_xgt, e + 1)
                    act.activation(xgm[u][:, :], B[5][:, 0:CAP], ACT.Copy).then_inc(s_xga, 1)

                def silu(e, u, n):
                    r = (ITEMS * u + n) % 2
                    act.wait_ge(s_gu, e * ITEMS + n + 1)
                    act.activation(sl[:, r, :, :], B[r][:, 0:2 * CAP].rearrange("p (m c) -> p m c", m=2),
                                   ACT.Silu).then_inc(s_silu, 1)

                def turn(i, u):
                    e = 2 * i + u
                    act.wait_ge(s_wd[u], 16 * i + 16)
                    if not isinstance(e, int) or e >= 2:
                        act.wait_ge(s_y, e - 1)
                    act.activation(wdh[u][:, :, :], wd[u][:, :, :], ACT.Copy).then_inc(s_wdh, 1)
                    silu(e, u, 0)
                    silu(e, u, 1)
                    if not isinstance(e, int) or e < E - 1:
                        tokens_main(e + 1, 1 - u)
                    silu(e, u, 2)

                tokens_main(0, 0)
                turn(0, 0)
                turn(0, 1)
                with act.Fori(1, E // 2 - 1) as i:
                    turn(i, 0)
                    turn(i, 1)
                turn(E // 2 - 1, 0)
                turn(E // 2 - 1, 1)

            @block.gpsimd
            def _(pool):
                def product(g, m):
                    pool.wait_ge(s_sga, g * KS + m + 1)
                    wait(pool, s_sd, g)
                    pool.tensor_tensor(sa[:, m, :], sgate[:, m, :], sup[:, m, :], ALU.mult).then_inc(s_sa, 1)

                def residual(g):
                    pool.wait_ge(s_sda, g * NT + NT)
                    pool.tensor_tensor(ysh[:, :, :], ysh[:, :, :], h_all[:, ds(g * NT, NT), :],
                                       ALU.add).then_inc(s_ysh, 1)

                for m in range(KS):
                    product(0, m)
                with pool.Fori(0, NG - 1) as g:
                    product(g + 1, 0)
                    residual(g)
                    product(g + 1, 1)
                    product(g + 1, 2)
                residual(NG - 1)
                pool.wait_ge(s_idx, 2)

                def carry_wait(n):
                    wait(pool, s_carry, n)
                    pool.tensor_tensor(pspare[:, 0:1], pspare[:, 1:2], pspare[:, 1:2], ALU.mult).then_inc(s_carry, 1)

                def gather(e, u, n):
                    if not isinstance(e, int) or e >= 2:
                        pool.wait_ge(s_xgt, e - 1)
                    pool.tensor_copy(idg[:, u, :], idx[:, :, ds(e, 1)].rearrange("p h a -> p (h a)")).then_inc(s_idg, 1)
                    pool.wait_ge(s_idg, e + 1)
                    carry_wait(n)
                    for h in range(2):
                        pool.indirect_dma_start(xg[u][:, h, :], None, x3_dram,
                                                bass.IndirectOffsetOnAxis(ap=idg[:, u, h:h + 1], axis=0)
                                                ).then_inc(s_gath[u], 16)

                def scatter(e, u, n):
                    pool.wait_ge(s_ys, 2 * e + 2)
                    wait(pool, s_scat, e * 32)
                    pool.tensor_copy(ids[:, u, :], idx[:, :, ds(e, 1)].rearrange("p h a -> p (h a)")).then_inc(s_ids, 1)
                    pool.wait_ge(s_ids, e + 1)
                    carry_wait(n)
                    for h in range(2):
                        pool.indirect_dma_start(out_rows, bass.IndirectOffsetOnAxis(ap=ids[:, u, h:h + 1], axis=0),
                                                ys[u][:, h, :], None, compute_op=ALU.add).then_inc(s_scat, 16)

                pool.wait_ge(s_x3out, 16 * NT * NG)
                gather(0, 0, 0)
                gather(1, 1, 1)
                gather(2, 0, 2)
                pool.wait_ge(s_init, NG * NT * 16)
                scatter(0, 0, 3)
                gather(3, 1, 4)
                with pool.Fori(1, E // 2 - 1) as i:
                    scatter(2 * i - 1, 1, 4 * i + 1)
                    gather(2 * i + 2, 0, 4 * i + 2)
                    scatter(2 * i, 0, 4 * i + 3)
                    gather(2 * i + 3, 1, 4 * i + 4)
                for e in range(E - 3, E):
                    scatter(e, e % 2, E + e)
                pool.wait_ge(s_scat, E * 32)

            @block.vector
            def _(dve):
                close(dve, Chain(dve, s_dve), NG - 1)
                dve.wait_ge(s_x3ps, 1)
                dve.tensor_copy(x3Tr[:, N - G:N], B[7][0:DR, 0:G]).then_inc(s_x3d, 1)
                first_picks = Pick(dve, scA, topsA, topiA, s_topA)
                first_picks.n = sum(PICKS_2 + PICKS_3)
                first_picks.steps(3 * ROUNDS - first_picks.n)
                dve.wait_ge(s_sc, NG + 1)
                Pick(dve, scB, topsB, topiB, s_top).steps(3 * ROUNDS)
                rev = slice(None, None, -1)
                dve.tensor_copy(idA, topiA)
                dve.tensor_copy(idB, topiB).then_inc(s_pick, 1)
                dve.tensor_tensor(isB, topsB[:, rev], topsA, ALU.is_gt).then_inc(s_pick, 1)
                dve.tensor_tensor(tops[:, :], topsA, topsB[:, rev], ALU.max).then_inc(s_pick, 1)
                dve.wait_ge(s_pick, 3)
                dve.scalar_tensor_tensor(diff, idB[:, rev], float(NA), idA, ALU.add, ALU.subtract).then_inc(s_pick, 1)
                dve.wait_ge(s_pick, 4)
                dve.tensor_tensor(diff, diff, isB, ALU.mult).then_inc(s_pick, 1)
                dve.wait_ge(s_pick, 5)
                dve.tensor_tensor(topf[:, :], diff, idA, ALU.add).then_inc(s_pick, 1)
                dve.wait_ge(s_topT, 1)
                dve.tensor_copy(idx[:, :, :], B[5][0:HC, 0:2 * E].rearrange("p (h e) -> p h e", h=2)).then_inc(s_idx, 1)
                dve.tensor_copy(scr[:, :, :], B[5][0:HC, 2 * E:4 * E].rearrange("p (h e) -> p h e", h=2)).then_inc(s_idx, 1)
                dve.wait_ge(s_idx, 2)

                def tokens_rest(e, u):
                    dve.wait_ge(s_xgt, e + 1)
                    dve.tensor_copy(xgr[u][:, :], B[4][0:DR, 0:CAP]).then_inc(s_xgd, 1)

                def product(e, u, n):
                    r = (ITEMS * u + n) % 2
                    dve.wait_ge(s_silu, e * ITEMS + n + 1)
                    dve.tensor_tensor(act32[:, r, :, :], B[2 + r][:, 0:2 * CAP].rearrange("p (m c) -> p m c", m=2),
                                      sl[:, r, :, :], ALU.mult).then_inc(s_prod, 1)
                    dve.wait_ge(s_prod, e * ITEMS + n + 1)
                    if n == 0 and (not isinstance(e, int) or e >= 2):
                        dve.wait_ge(s_y, e - 1)
                    high = ah[u][:, 2 * n:2 * n + 2, :]
                    dve.tensor_copy(high, act32[:, r, :, :]).then_inc(s_ah, 1)
                    dve.wait_ge(s_ah, e * ITEMS + n + 1)
                    dve.tensor_tensor(al[u][:, 2 * n:2 * n + 2, :], act32[:, r, :, :], high.bitcast(F32),
                                      ALU.subtract).then_inc(s_act, 1)

                def weighted(e, u):
                    dve.wait_ge(s_y, e + 1)
                    if not isinstance(e, int) or e >= 2:
                        dve.wait_ge(s_scat, 32 * (e - 1))
                    for h in range(2):
                        dve.tensor_scalar(ys[u][:, h, :], B[6 + u][0:HC, h * 256:h * 256 + D],
                                          scr[:, h, ds(e, 1)], None, ALU.mult).then_inc(s_ys, 1)

                def turn(i, u):
                    e = 2 * i + u
                    product(e, u, 0)
                    dve.wait_ge(s_wdh, e + 1)
                    dve.tensor_tensor(wdl[u][:, :, :], wd[u][:, :, :], wdh[u][:, :, :].bitcast(F32),
                                      ALU.subtract).then_inc(s_wdl, 1)
                    if not isinstance(e, int) or e > 0:
                        weighted(e - 1, 1 - u)
                    product(e, u, 1)
                    if not isinstance(e, int) or e < E - 1:
                        tokens_rest(e + 1, 1 - u)
                    product(e, u, 2)

                tokens_rest(0, 0)
                turn(0, 0)
                turn(0, 1)
                with dve.Fori(1, E // 2 - 1) as i:
                    turn(i, 0)
                    turn(i, 1)
                turn(E // 2 - 1, 0)
                turn(E // 2 - 1, 1)
                weighted(E - 1, 1)


def kernel(**inputs):
    import numpy as _np
    import concourse.bacc as _bacc
    from concourse import mybir as _mybir
    from concourse.bass_utils import run_bass_kernel_spmd as _run

    a = {k: _np.asarray(v) for k, v in inputs.items()}
    x = a["x"].reshape(IMAGES, 3, 6, PATCH, 6, PATCH).transpose(0, 2, 4, 1, 3, 5).reshape(NG, G, KI, 128)
    Wq, Wk, Wv = _np.split(a["L0_attn_W_qkv"], 3, axis=1)
    bq, bk, bv = _np.split(a["L0_attn_b_qkv"], 3)

    def tiles(w):
        w = w.reshape(-1, 4, 2, D)
        rest = w[:, :, :, DM:].reshape(-1, 4, 1, 128)
        return _np.concatenate([rest, w[:, :, :, :DM]], axis=2).reshape(-1, 12, 128)

    rows = _np.arange(PAIR) < PAIR // 2
    blocks = _np.zeros((2, 2 * PAIR), _np.float32)
    blocks[0, :PAIR], blocks[1, :PAIR] = rows, ~rows
    blocks[0, PAIR:], blocks[1, PAIR:] = _np.where(~rows, -1e30, 0), _np.where(rows, -1e30, 0)
    arrays = {
        "xT": x.transpose(0, 3, 2, 1),
        "W1": a["L0_tok_W1"].reshape(KI, 128, KH, 128).transpose(2, 1, 0, 3),
        "b1": a["L0_tok_b1"].reshape(KH, 128).T,
        "W2": a["L0_tok_W2"].reshape(KH, 128, D).transpose(1, 0, 2),
        "b2": a["L0_tok_b2"],
        "Wqp": _np.concatenate([tiles(Wq).reshape(D, QKV), tiles(Wk).reshape(D, QKV),
                                a["L0_attn_W_proj"].reshape(HEADS, D, D).transpose(1, 0, 2).reshape(D, QKV)], axis=1),
        "bqk": _np.concatenate([tiles(bq), tiles(bk)], axis=1)[0].T,
        "Wv": Wv, "bv": bv,
        "bp": a["L0_attn_b_proj"],
        "blocks": blocks,
        "gateT": a["L0_ffn_gate_weight"].T,
        "Wgu": _np.concatenate([a["L0_ffn_Wg"].transpose(0, 2, 1), a["L0_ffn_Wu"].transpose(0, 2, 1)], axis=2),
        "Wd": a["L0_ffn_Wd"].transpose(0, 2, 1).reshape(E, KF, 128, D).transpose(0, 2, 1, 3),
        "Wsgu": _np.concatenate([a["L0_ffn_Ws_g"].T, a["L0_ffn_Ws_u"].T], axis=1),
        "Wsd": a["L0_ffn_Ws_d"].T.reshape(KS, 128, D).transpose(1, 0, 2),
    }
    nc = _bacc.Bacc("TRN2", target_bir_lowering=False, num_devices=1)
    feed, args = {}, []
    for name, v in arrays.items():
        v = _np.ascontiguousarray(v)
        feed[f"in_{name}"] = v
        args.append(nc.dram_tensor(f"in_{name}", v.shape, _mybir.dt.from_np(v.dtype), kind="ExternalInput").ap())
    args.append(nc.dram_tensor("out_0", (IMAGES, SEQ, D), _mybir.dt.float32, kind="ExternalOutput").ap())
    vit_moe_kernel(nc, *args)
    r = _run(nc, [feed], core_ids=[0])
    return r.results[0]["out_0"]
```
